# Optimizing a Trainium2 kernel written in Bass

```python
import numpy as np
import jax
import jax.numpy as jnp

def _softmax(x, axis=-1):
    return jax.nn.softmax(x, axis=axis)

def _gelu(x):
    return jax.nn.gelu(x, approximate=True)

def _silu(x):
    return jax.nn.silu(x)

def _sigmoid(x):
    return jax.nn.sigmoid(x)

def _layernorm(x, axis=-1, eps=1e-05):
    m = jnp.mean(x, axis=axis, keepdims=True)
    v = jnp.var(x, axis=axis, keepdims=True)
    return (x - m) / jnp.sqrt(v + eps)

def _scatter_add(tgt, idx, src, axis=0):
    return tgt.at[idx].add(src)

def _segment_sum(src, seg, n):
    return jax.ops.segment_sum(src, seg, n)
kernel_name = 'mk_macaron_d1_jaxref_r8_788876'

def setup_inputs(seed: int=0):
    np.random.seed(seed)
    _w = jnp.asarray

    def _L0_attn_setup():
        import jax, jax.numpy as jnp
        import numpy as np
        B, L, D, H = (4, 512, 256, 16)
        HD = D // H
        EPS = 1e-09

        def phi(x):
            return jax.nn.elu(x) + 1.0
        key = jax.random.key(seed)
        k1, k2, k3 = jax.random.split(key, 3)
        x = jax.random.normal(k1, (B, L, D), dtype=jnp.float32)
        W_qkv = jax.random.normal(k2, (3 * D, D), dtype=jnp.float32) * D ** (-0.5)
        W_out = jax.random.normal(k3, (D, D), dtype=jnp.float32) * D ** (-0.5)
        return {'x': x, 'W_qkv': W_qkv, 'W_out': W_out}
    _L0_attn_in = _L0_attn_setup()

    def _L0_ffn_setup():
        import jax, jax.numpy as jnp
        import numpy as np
        B, S, D = (2, 256, 256)
        H, HD = (16, 128)
        E, K, I = (16, 6, 176)
        SI = 352
        EPS = 1e-06

        def rmsnorm(x, w):
            v = jnp.mean(jnp.square(x), axis=-1, keepdims=True)
            return x * jax.lax.rsqrt(v + EPS) * w
        key = jax.random.key(seed)
        ks = jax.random.split(key, 14)
        s = 0.02
        return {'hidden_states': jax.random.normal(ks[0], (B, S, D), jnp.float32), 'ln1_w': jnp.ones((D,), jnp.float32), 'ln2_w': jnp.ones((D,), jnp.float32), 'wq': jax.random.normal(ks[1], (D, H * HD), jnp.float32) * s, 'wk': jax.random.normal(ks[2], (D, H * HD), jnp.float32) * s, 'wv': jax.random.normal(ks[3], (D, H * HD), jnp.float32) * s, 'wo': jax.random.normal(ks[4], (H * HD, D), jnp.float32) * s, 'gate_w': jax.random.normal(ks[5], (E, D), jnp.float32) * s, 'eg_w': jax.random.normal(ks[6], (E, I, D), jnp.float32) * s, 'eu_w': jax.random.normal(ks[7], (E, I, D), jnp.float32) * s, 'ed_w': jax.random.normal(ks[8], (E, D, I), jnp.float32) * s, 'sg_w': jax.random.normal(ks[9], (SI, D), jnp.float32) * s, 'su_w': jax.random.normal(ks[10], (SI, D), jnp.float32) * s, 'sd_w': jax.random.normal(ks[11], (D, SI), jnp.float32) * s}
    _L0_ffn_in = _L0_ffn_setup()
    _d = {'L0_attn_x': _L0_attn_in['x'], 'L0_attn_W_qkv': _L0_attn_in['W_qkv'], 'L0_attn_W_out': _L0_attn_in['W_out'], 'L0_ffn_ln1_w': _L0_ffn_in['ln1_w'], 'L0_ffn_ln2_w': _L0_ffn_in['ln2_w'], 'L0_ffn_wq': _L0_ffn_in['wq'], 'L0_ffn_wk': _L0_ffn_in['wk'], 'L0_ffn_wv': _L0_ffn_in['wv'], 'L0_ffn_wo': _L0_ffn_in['wo'], 'L0_ffn_gate_w': _L0_ffn_in['gate_w'], 'L0_ffn_eg_w': _L0_ffn_in['eg_w'], 'L0_ffn_eu_w': _L0_ffn_in['eu_w'], 'L0_ffn_ed_w': _L0_ffn_in['ed_w'], 'L0_ffn_sg_w': _L0_ffn_in['sg_w'], 'L0_ffn_su_w': _L0_ffn_in['su_w'], 'L0_ffn_sd_w': _L0_ffn_in['sd_w']}
    _x0 = _d['L0_attn_x']
    _d['L0_attn_x'] = jax.random.normal(jax.random.fold_in(jax.random.key(seed), 1), (4, 256, 256), dtype=_x0.dtype)
    del _x0
    return _d

def reference(L0_attn_x, L0_attn_W_qkv, L0_attn_W_out, L0_ffn_ln1_w, L0_ffn_ln2_w, L0_ffn_wq, L0_ffn_wk, L0_ffn_wv, L0_ffn_wo, L0_ffn_gate_w, L0_ffn_eg_w, L0_ffn_eu_w, L0_ffn_ed_w, L0_ffn_sg_w, L0_ffn_su_w, L0_ffn_sd_w):

    def _L0_attn_ref(x, W_qkv, W_out):
        import jax, jax.numpy as jnp
        import numpy as np
        B, L, D, H = (4, 512, 256, 16)
        HD = D // H
        EPS = 1e-09

        def phi(x):
            return jax.nn.elu(x) + 1.0
        b, l, d = x.shape
        qkv = x @ W_qkv.T
        q, k, v = jnp.split(qkv, 3, axis=-1)
        q = q.reshape(b, l, H, HD).transpose(0, 2, 1, 3)
        k = k.reshape(b, l, H, HD).transpose(0, 2, 1, 3)
        v = v.reshape(b, l, H, HD).transpose(0, 2, 1, 3)
        q = phi(q)
        k = phi(k)
        kv_cumsum = jnp.cumsum(k * v, axis=2)
        k_cumsum = jnp.cumsum(k, axis=2)
        out = q * kv_cumsum / (q * k_cumsum + EPS)
        out = out.transpose(0, 2, 1, 3).reshape(b, l, d)
        return out @ W_out.T * HD ** (-0.5)

    def _L0_ffn_ref(hidden_states, ln1_w, ln2_w, wq, wk, wv, wo, gate_w, eg_w, eu_w, ed_w, sg_w, su_w, sd_w):
        import jax, jax.numpy as jnp
        import numpy as np
        B, S, D = (2, 256, 256)
        H, HD = (16, 128)
        E, K, I = (16, 6, 176)
        SI = 352
        EPS = 1e-06

        def rmsnorm(x, w):
            v = jnp.mean(jnp.square(x), axis=-1, keepdims=True)
            return x * jax.lax.rsqrt(v + EPS) * w
        b, s, d = hidden_states.shape
        x = hidden_states
        h = rmsnorm(x, ln1_w)
        q = (h @ wq).reshape(b, s, H, HD)
        k = (h @ wk).reshape(b, s, H, HD)
        v = (h @ wv).reshape(b, s, H, HD)
        scores = jnp.einsum('bqhd,bkhd->bhqk', q, k) / np.sqrt(HD).astype(np.float32)
        causal = jnp.tril(jnp.ones((s, s), bool))
        scores = jnp.where(causal, scores, jnp.float32(-1000000000.0))
        attn = jax.nn.softmax(scores, axis=-1)
        ao = jnp.einsum('bhqk,bkhd->bqhd', attn, v).reshape(b, s, H * HD) @ wo
        x = x + ao
        h = rmsnorm(x, ln2_w)
        t = h.reshape(-1, d)
        T = t.shape[0]
        logits = t @ gate_w.T
        probs = jax.nn.softmax(logits, axis=-1)
        topv, topi = jax.lax.top_k(probs, K)
        topv = topv / jnp.sum(topv, axis=-1, keepdims=True)
        cw = jnp.zeros((T, E), t.dtype).at[jnp.arange(T)[:, None], topi].add(topv)
        g = jnp.einsum('td,eid->eti', t, eg_w)
        u = jnp.einsum('td,eid->eti', t, eu_w)
        hh = jax.nn.silu(g) * u
        routed = jnp.einsum('eti,edi,te->td', hh, ed_w, cw)
        shared = jax.nn.silu(t @ sg_w.T) * (t @ su_w.T) @ sd_w.T
        out = x + (routed + shared).reshape(b, s, d)
        return out
    x = L0_attn_x
    x = x + 0.5 * _L0_ffn_ref(_layernorm(x, axis=-1), L0_ffn_ln1_w, L0_ffn_ln2_w, L0_ffn_wq, L0_ffn_wk, L0_ffn_wv, L0_ffn_wo, L0_ffn_gate_w, L0_ffn_eg_w, L0_ffn_eu_w, L0_ffn_ed_w, L0_ffn_sg_w, L0_ffn_su_w, L0_ffn_sd_w)
    x = x + _L0_attn_ref(_layernorm(x, axis=-1), L0_attn_W_qkv, L0_attn_W_out)
    x = x + 0.5 * _L0_ffn_ref(_layernorm(x, axis=-1), L0_ffn_ln1_w, L0_ffn_ln2_w, L0_ffn_wq, L0_ffn_wk, L0_ffn_wv, L0_ffn_wo, L0_ffn_gate_w, L0_ffn_eg_w, L0_ffn_eu_w, L0_ffn_ed_w, L0_ffn_sg_w, L0_ffn_su_w, L0_ffn_sd_w)
    return x

_drawn_inputs = setup_inputs


def setup_inputs(seed=0):
    import zlib

    import numpy as np

    out = dict(_drawn_inputs(seed))
    spreads = {'L0_ffn_ln1_w': (1.0, 0.6), 'L0_ffn_ln2_w': (1.0, 0.6)}
    factors = {'L0_ffn_wq': 8.0,
     'L0_ffn_wk': 8.0,
     'L0_ffn_gate_w': 8.0,
     'L0_ffn_eg_w': 8.0,
     'L0_ffn_eu_w': 8.0,
     'L0_ffn_ed_w': 8.0,
     'L0_ffn_sg_w': 4.391,
     'L0_ffn_su_w': 4.332,
     'L0_ffn_sd_w': 4.31,
     'L0_attn_W_qkv': 2.967,
     'L0_attn_W_out': 2.791}
    for name, (base, spread) in spreads.items():
        noise = np.random.default_rng([zlib.crc32(name.encode()), seed]).standard_normal(out[name].shape)
        drawn = base * np.exp(spread * noise) if base else spread * noise
        out[name] = jnp.asarray(drawn.astype(out[name].dtype))
    for name, factor in factors.items():
        out[name] = (out[name] * factor).astype(out[name].dtype)
    return out
```

```python
import numpy as np
import concourse.bass as bass
from concourse import mybir
from contextlib import ExitStack

F32 = mybir.dt.float32
F32R = mybir.dt.float32r
BF16 = mybir.dt.bfloat16
I32 = mybir.dt.int32
ALU = mybir.AluOpType
ACT = mybir.ActivationFunctionType
X_AXIS = mybir.AxisListType.X

P = 128
T, D = 1024, 256
NT, DC = T // P, D // P
NB, S = 4, 256
H, HD = 16, 128
PAIRS = H // 2
E, I, SI, TOPK = 16, 176, 352, 6
EROWS = 32
UP = E * I + SI
NCH = -(-UP // P)
HALF = 512
SCALE = float(HD) ** -0.5
GLA_SCALE = float(D // 16) ** -0.5
LN_EPS, RMS_EPS, GLA_EPS = 1e-5, 1e-6, 1e-9
QKW, WOW = 2 * D, D
MW = 3 * D
ITEMS = H * NB
UNITS = 2 * NCH
MAGIC = 1597463007.0


def program(nc, x_in, wqk_in, wo_in, wv_in, moe_in, gate_in, ln_in, wqkv_in, wout_in,
            ident_in, identb_in, mask_in, seg_in, sel_in, out):
    ctx = ExitStack()
    with ctx:
        def sb(name, cols, dt, parts=P):
            return ctx.enter_context(nc.sbuf_tensor(name, [parts, cols], dt))

        def sem(name):
            return ctx.enter_context(nc.semaphore(name))

        X = sb("X", NT * D, F32)
        Y = sb("Y", NT * D, F32)
        big = sb("big", NT * H * HD, F32)
        Z = big[:, 0:NT * D]
        silu_t = [big[:, 2048 + 512 * s:2560 + 512 * s] for s in range(2)]
        su_t = big[:, 3072:3584]
        hw_t = [big[:, 3584 + 512 * s:4096 + 512 * s] for s in range(2)]
        prob = big[:, 4608:4736]
        gt_t, eq_t, inc_t, sel_t = (big[:, 4736 + 128 * s:4864 + 128 * s] for s in range(4))
        rest1 = big[:, 5248:5504]
        rest2 = big[:, 5504:5760]
        cw = big[:, 5760:6016]
        cw3 = big[:, 6016:6400].bitcast(BF16)
        cwT = big[0:3 * EROWS, 6400:6912].bitcast(BF16)
        squared = big[:, 7168:9216]
        g_e, g_r = big[:, 2048:4096], big[:, 4096:6144]
        g_k, g_q, g_kv = big[:, 6144:8192], big[:, 8192:10240], big[:, 10240:12288]
        g_kc, g_kvc = big[:, 12288:14336], big[:, 14336:16384]
        v3 = big[:, :].rearrange("p (n f) -> p n f", n=NT)

        hTh, hTl = sb("hTh", DC * T, F32R), sb("hTl", DC * T, F32R)
        Wh, Wl = sb("Wh", 2 * MW, F32R), sb("Wl", 2 * MW, F32R)
        QK = sb("QK", 8 * T, F32R)
        Vs = sb("Vs", 4 * T, F32R)
        PT = sb("PT", 4 * 384, F32R)
        CA = sb("CA", 2 * T, F32R)
        CB = sb("CB", 4 * S, F32R)
        SP_ = sb("SP_", 6 * 384, F32)
        raw_qk, raw_wo = sb("raw_qk", 2 * QKW, F32), sb("raw_wo", 2 * WOW, F32)
        raw_moe = sb("raw_moe", 2 * MW, F32)
        ident, identb = sb("ident", P, F32), sb("identb", P, BF16)
        mask, seg = sb("mask", 384, F32), sb("seg", P, F32)
        sel = sb("sel", NCH * P, BF16, 3 * EROWS)
        lnw = sb("lnw", 2 * DC, F32)
        graw = sb("graw", DC * E, F32)
        gwh, gwl = sb("gwh", DC * E, F32R), sb("gwl", DC * E, F32R)
        stats, mv = sb("stats", NT * 6, F32), sb("mv", NT * 2, F32)
        ss = sb("ss", NT, F32)
        rstd, rv, ry, rt = (sb(n, NT, F32) for n in ("rstd", "rv", "ry", "rt"))
        nmax, rsum, rinv = (sb(n, 8, F32) for n in ("nmax", "rsum", "rinv"))
        mx8, sm8, rs8, cg8 = (sb(n, NT, F32) for n in ("mx8", "sm8", "rs8", "cg8"))
        top8 = sb("top8", NT * 8, F32)

        bank = [ctx.enter_context(nc.psum_tensor(f"bank{i}", [P, 512], F32)) for i in range(8)]

        def q_h(s): return QK[:, 4096 * s:4096 * s + 1024]
        def q_l(s): return QK[:, 4096 * s + 1024:4096 * s + 2048]
        def k_h(s): return QK[:, 4096 * s + 2048:4096 * s + 3072]
        def k_l(s): return QK[:, 4096 * s + 3072:4096 * s + 4096]
        def v_h(s): return Vs[:, 2048 * s:2048 * s + 1024]
        def v_l(s): return Vs[:, 2048 * s + 1024:2048 * s + 2048]
        def sc(j): return SP_[:, 384 * (j % 2):384 * (j % 2) + 384]
        def pr(j): return SP_[:, 384 * (2 + j % 4):384 * (2 + j % 4) + 384]
        def pt_h(j): return PT[:, 768 * (j % 2):768 * (j % 2) + 384]
        def pt_l(j): return PT[:, 768 * (j % 2) + 384:768 * (j % 2) + 768]
        def ring(s, a, n): return Wh[:, MW * s + a:MW * s + a + n], Wl[:, MW * s + a:MW * s + a + n]
        hh_h = [CA[:, 1024 * s:1024 * s + 512] for s in range(2)]
        hh_l = [CA[:, 1024 * s + 512:1024 * s + 1024] for s in range(2)]

        def ctx_slot(s):
            if s < 4:
                return CA[:, S * s:S * s + S], CA[:, 1024 + S * s:1024 + S * s + S]
            c = 2 * S * (s % 2)
            return CB[:, c:c + S], CB[:, c + S:c + 2 * S]

        ld_x = [sem(f"ld_x{n}") for n in range(2)]
        ld_const, ld_sel = sem("ld_const"), sem("ld_sel")
        ld_wv = [sem(f"ld_wv{s}") for s in range(2)]
        ld_qk = [sem(f"ld_qk{s}") for s in range(2)]
        ld_wo = [sem(f"ld_wo{s}") for s in range(2)]
        ld_moe = [sem(f"ld_moe{s}") for s in range(2)]
        ld_gqkv, ld_gout = sem("ld_gqkv"), sem("ld_gout")
        stored = sem("stored")
        pool_passed, dve_passed = sem("pool_passed"), sem("dve_passed")
        dve_step = sem("dve_step")
        y_ready, ss_ready, z_ready = sem("y_ready"), sem("ss_ready"), sem("z_ready")
        zT_done, hT_hi, hT_ready = sem("zT_done"), sem("hT_hi"), sem("hT_ready")
        wv_hi, wv_ready = sem("wv_hi"), sem("wv_ready")
        wqk_hi, wqk_ready = sem("wqk_hi"), sem("wqk_ready")
        wo_hi, wo_ready = sem("wo_hi"), sem("wo_ready")
        moe_hi, moe_ready = sem("moe_hi"), sem("moe_ready")
        gw_hi, gw_ready = sem("gw_hi"), sem("gw_ready")
        gla_hi, gla_w_ready = sem("gla_hi"), sem("gla_w_ready")
        v_done, v_saved_act, v_saved_dve = sem("v_done"), sem("v_saved_act"), sem("v_saved_dve")
        vs_hi, vs_ready = sem("vs_hi"), sem("vs_ready")
        proj_done, proj_hi, proj_ready = sem("proj_done"), sem("proj_hi"), sem("proj_ready")
        scores_done, masked = sem("scores_done"), sem("masked")
        exp_done, rinv_ready, probs_ready = sem("exp_done"), sem("rinv_ready"), sem("probs_ready")
        probsT_done, pt_hi, pt_ready = sem("probsT_done"), sem("pt_hi"), sem("pt_ready")
        ctx_done, ctx_hi, ctx_ready = sem("ctx_done"), sem("ctx_hi"), sem("ctx_ready")
        wo_done, wo_added = sem("wo_done"), sem("wo_added")
        logits_done, lshift, lexp = sem("logits_done"), sem("lshift"), sem("lexp")
        cw3_ready, cwT_done, cwT_ready = sem("cw3_ready"), sem("cwT_done"), sem("cwT_ready")
        y_halved, x_half = sem("y_halved"), sem("x_half")
        g_done, silu_ready, u_done, su_ready = (
            sem("g_done"), sem("silu_ready"), sem("u_done"), sem("su_ready"))
        cwb_done, hw_ready, hh_hi_ready, hh_ready = (
            sem("cwb_done"), sem("hw_ready"), sem("hh_hi_ready"), sem("hh_ready"))
        down_done, x_moe = sem("down_done"), sem("x_moe")
        gu_done, gu_act, gu_phi, gu_kv = sem("gu_done"), sem("gu_act"), sem("gu_phi"), sem("gu_kv")
        go_ready, go_hi, go_lo = sem("go_ready"), sem("go_hi"), sem("go_lo")
        gout_done, gout_added = sem("gout_done"), sem("gout_added")
        block = ctx.enter_context(nc.Block())


        def after(eng, sm, value):
            if not isinstance(value, int) or value > 0:
                eng.wait_ge(sm, value)

        def after_alone(eng, sm, value, passed):
            if not isinstance(value, int) or value > 0:
                eng.wait_ge(sm, value)
                eng.sem_inc(passed, 1)

        def over_pairs(eng, body):
            body(0)
            with eng.Fori(1, PAIRS - 1) as i:
                body(i)
            body(PAIRS - 1)

        def is_(i, value):
            return isinstance(i, int) and i == value

        GU = [(u // 6, (u % 6) // 2, u % 2) for u in range(12)]
        kq_before = [sum(GU[w][1] < 2 for w in range(u)) for u in range(13)]
        v_before = [u - kq_before[u] for u in range(13)]

        @block.sync
        def _(sp):
            for n in range(2):
                sp.dma_start(X[:, 1024 * n:1024 * n + 1024].rearrange("p (n d) -> p n d", n=4),
                             x_in[:, 4 * n:4 * n + 4, :]).then_inc(ld_x[n], 16)
            for dst, src in ((ident, ident_in), (lnw, ln_in), (graw, gate_in), (identb, identb_in),
                             (mask, mask_in), (seg, seg_in)):
                sp.dma_start(dst[:, :], src).then_inc(ld_const, 16)

            def head(src, g):
                return src[bass.ds(g, 1), :, :].rearrange("a p f -> (a p) f")

            def qk(L, i, s):
                after(sp, wqk_ready, L * H + 2 * (i - 1) + s + 1)
                sp.dma_start(raw_qk[:, QKW * s:QKW * s + QKW], head(wqk_in, 2 * i + s))\
                    .then_inc(ld_qk[s], 16)

            def wo(L, i, s):
                after(sp, wo_ready, L * H + 2 * (i - 1) + s + 1)
                sp.dma_start(raw_wo[:, WOW * s:WOW * s + WOW], head(wo_in, 2 * i + s))\
                    .then_inc(ld_wo[s], 16)

            def chunk(L, c, s):
                after(sp, moe_ready, 2 * (L * NCH + c - 1))
                sp.dma_start(raw_moe[:, MW * s:MW * s + MW], head(moe_in, c))\
                    .then_inc(ld_moe[s], 16)

            for L in range(2):
                if L:
                    sp.wait_ge(probsT_done, ITEMS)
                for cb in range(4):
                    if cb >= 2:
                        sp.wait_ge(wv_ready, 4 * L + cb - 1)
                    s = cb % 2
                    sp.dma_start(SP_[:, 1024 * s:1024 * s + 1024].rearrange("p (c f) -> p c f", c=DC),
                                 wv_in[:, :, 512 * cb:512 * cb + 512]).then_inc(ld_wv[s], 16)
                    if cb == 1:
                        qk(L, 0, 0)
                        qk(L, 0, 1)
                if L == 0:
                    sp.dma_start(sel[:, :], sel_in).then_inc(ld_sel, 16)
                else:
                    sp.wait_ge(gla_w_ready, 2)

                def pair(i):
                    for s in range(2):
                        wo(L, i, s)
                    if not is_(i, PAIRS - 1):
                        for s in range(2):
                            qk(L, i + 1, s)

                over_pairs(sp, pair)
                if L:
                    sp.wait_ge(gla_w_ready, 1)
                for c in range(3):
                    chunk(L, c, c % 2)
                with sp.Fori(1, NCH // 2) as r:
                    chunk(L, 2 * r + 1, 1)
                    chunk(L, 2 * r + 2, 0)
                if L == 0:
                    sp.wait_ge(wo_ready, H)
                    sp.dma_start(raw_wo[:, :], wout_in).then_inc(ld_gout, 16)
                    sp.wait_ge(moe_ready, 2 * NCH)
                    sp.dma_start(raw_moe[:, :], wqkv_in).then_inc(ld_gqkv, 16)
            for q in range(4):
                sp.wait_ge(x_moe, 4 + q + 1)
                sp.dma_start(out[:, 2 * q:2 * q + 2, :],
                             X[:, 512 * q:512 * q + 512].rearrange("p (n d) -> p n d", n=2))\
                    .then_inc(stored, 16)
            sp.wait_ge(stored, 16 * 4)

        @block.gpsimd
        def _(pool):
            def split(hi, lo, raw, hi_sem, hi_count, lo_sem):
                nc.gpsimd.tensor_scalar(hi, raw, 1.0, 1.0, ALU.mult, ALU.mult).then_inc(hi_sem, 1)
                pool.wait_ge(hi_sem, hi_count)
                nc.gpsimd.tensor_tensor(lo, raw, hi.bitcast(F32), ALU.subtract).then_inc(lo_sem, 1)

            def qk_split(L, i, s):
                after_alone(pool, ld_qk[s], 16 * (L * PAIRS + i + 1), pool_passed)
                after_alone(pool, proj_done, L * ITEMS + 8 * (i - 1) + 4 * s + 4, pool_passed)
                split(*ring(s, 0, QKW), raw_qk[:, QKW * s:QKW * s + QKW],
                      wqk_hi, L * H + 2 * i + s + 1, wqk_ready)

            def wo_split(L, i, s):
                after_alone(pool, ld_wo[s], 16 * (L * PAIRS + i + 1), pool_passed)
                after_alone(pool, wo_done, L * 4 * PAIRS + 4 * i, pool_passed)
                split(*ring(s, QKW, WOW), raw_wo[:, WOW * s:WOW * s + WOW],
                      wo_hi, L * H + 2 * i + s + 1, wo_ready)

            def v_low(L, i, s):
                pool.wait_ge(vs_hi, L * H + 2 * i + s + 1)
                nc.gpsimd.tensor_tensor(
                    v_l(s).rearrange("p (n f) -> p n f", n=NT),
                    v3[:, :, bass.ds(HD * (2 * i + s), HD)],
                    v_h(s).bitcast(F32).rearrange("p (n f) -> p n f", n=NT),
                    ALU.subtract).then_inc(vs_ready, 1)

            def normalise(L, i, s):
                after_alone(pool, rinv_ready, L * ITEMS + 8 * i + s + 1, pool_passed)
                for t, (a, b) in enumerate(((0, P), (P, 3 * P))):
                    q = 2 * (s % 4) + t
                    last = nc.gpsimd.tensor_scalar(pr(s)[:, a:b], pr(s)[:, a:b], rinv[:, q:q + 1],
                                                   1.0, ALU.mult, ALU.mult)
                last.then_inc(probs_ready, 1)

            def moe_chunk(L, c, s, load):
                after_alone(pool, ld_moe[s], 16 * load, pool_passed)
                raw = raw_moe[:, MW * s:MW * s + MW]
                after_alone(pool, u_done, L * UNITS + 2 * c - 2, pool_passed)
                split(*ring(s, 0, 2 * D), raw[:, 0:2 * D], moe_hi, 2 * (L * NCH + c) + 1, moe_ready)
                after_alone(pool, down_done, L * UNITS + 2 * c - 2, pool_passed)
                split(*ring(s, 2 * D, D), raw[:, 2 * D:MW], moe_hi, 2 * (L * NCH + c) + 2, moe_ready)

            for L in range(2):
                if L:
                    pool.wait_ge(gout_done, 4)
                for cb in range(4):
                    pool.wait_ge(ld_wv[cb % 2], 16 * (2 * L + cb // 2 + 1))
                    raw = SP_[:, 1024 * (cb % 2):1024 * (cb % 2) + 1024]
                    split(QK[:, 2048 * cb:2048 * cb + 1024], QK[:, 2048 * cb + 1024:2048 * cb + 2048],
                          raw, wv_hi, 4 * L + cb + 1, wv_ready)
                if L:
                    pool.wait_ge(down_done, UNITS)
                qk_split(L, 0, 0)
                qk_split(L, 0, 1)
                if L == 0:
                    pool.wait_ge(ld_const, 16 * 6)
                    split(gwh[:, :], gwl[:, :], graw[:, :], gw_hi, 1, gw_ready)

                def pair(i):
                    for s in range(8):
                        if s > 0:
                            normalise(L, i, s - 1)
                        elif not is_(i, 0):
                            normalise(L, i - 1, 7)
                        if s == 0:
                            v_low(L, i, 0)
                        if s == 1 and not is_(i, PAIRS - 1):
                            qk_split(L, i + 1, 0)
                        if s == 3:
                            v_low(L, i, 1)
                        if s == 5 and not is_(i, PAIRS - 1):
                            qk_split(L, i + 1, 1)
                        if s >= 6:
                            wo_split(L, i, s - 6)

                over_pairs(pool, pair)
                normalise(L, PAIRS - 1, 7)

                pool.wait_ge(wo_done, (L + 1) * 4 * PAIRS)
                even, odd = NCH // 2 + 1, NCH // 2
                moe_chunk(L, 0, 0, L * even + 1)
                pool.wait_ge(z_ready, NT * (3 * L + 2))
                nc.gpsimd.tensor_scalar(Y[:, :], Y[:, :], 0.5, 1.0, ALU.mult, ALU.mult)\
                    .then_inc(y_halved, 1)
                pool.wait_ge(y_halved, L + 1)
                nc.gpsimd.tensor_tensor(X[:, :], X[:, :], Y[:, :], ALU.add).then_inc(x_half, 1)
                moe_chunk(L, 1, 1, L * odd + 1)
                moe_chunk(L, 2, 0, L * even + 2)
                with pool.Fori(1, NCH // 2) as r:
                    moe_chunk(L, 2 * r + 1, 1, r + (L * odd + 1))
                    moe_chunk(L, 2 * r + 2, 0, r + (L * even + 2))
                if L == 0:
                    pool.wait_ge(ld_gqkv, 16)
                    split(QK[:, 0:1536], QK[:, 1536:3072], raw_moe[:, :], gla_hi, 1, gla_w_ready)
                    pool.wait_ge(ld_gout, 16)
                    split(QK[:, 3072:3584], QK[:, 3584:4096], raw_wo[:, :], gla_hi, 2, gla_w_ready)

        @block.scalar
        def _(act):
            def squares(L, first):
                for n in range(NT):
                    if first:
                        act.wait_ge(y_ready, NT * L + n + 1)
                    else:
                        act.wait_ge(wo_added, 4 * PAIRS * L + 4 * (PAIRS - 1) + n // 2 + 1)
                    nc.scalar.activation(squared[:, D * n:D * n + D], Y[:, D * n:D * n + D], ACT.Square,
                                         accum_out=ss[:, n:n + 1]).then_inc(ss_ready, 1)

            def hT_high(k):
                for q in range(4):
                    hf, c = q // 2, q % 2
                    w = {0: 0, 1: DC, 3: 0, 4: DC}.get(k)
                    act.wait_ge(zT_done, 4 * k + q + 1)
                    o = hTh[:, T * c + HALF * hf:T * c + HALF * hf + HALF]
                    nc.scalar.activation(o, bank[q][:, :], ACT.Copy,
                                         scale=1.0 if w is None else lnw[:, w + c:w + c + 1])\
                        .then_inc(hT_hi, 1)

            act.wait_ge(ld_const, 16 * 6)
            for L in range(2):
                squares(L, True)
                hT_high(3 * L)

                def v_block(cb):
                    for n in range(0, NT, 2):
                        act.wait_ge(v_done, L * 4 * NT + 8 * cb + n + 1)
                        nc.scalar.activation(v3[:, n, bass.ds(512 * cb, 512)],
                                             bank[4 + n % 4][:, :], ACT.Copy).then_inc(v_saved_act, 1)
                with act.Fori(0, 4) as cb:
                    v_block(cb)

                def proj_high(i, s):
                    act.wait_ge(proj_done, L * ITEMS + 8 * i + 4 + s + 1)
                    q_or_k = (q_h, k_h)[s % 2](0 if s >= 4 else 1)
                    hf = (s % 4) // 2
                    nc.scalar.activation(q_or_k[:, HALF * hf:HALF * hf + HALF], bank[s % 2][:, :],
                                         ACT.Copy).then_inc(proj_hi, 1)

                def v_high(i, s):
                    g = 2 * i + s
                    after(act, ctx_done, L * ITEMS + 8 * (i - 1) + 4 * s + 4)
                    nc.scalar.activation(v_h(s).rearrange("p (n f) -> p n f", n=NT),
                                         v3[:, :, bass.ds(HD * g, HD)], ACT.Copy).then_inc(vs_hi, 1)

                def step(i, s, late=False):
                    j = 8 * i + s
                    if not (is_(i, 0) and s < 2) and not (late and s >= 2):
                        act.wait_ge(probsT_done, L * ITEMS + j - 1)
                        after(act, ctx_done, L * ITEMS + j - 3)
                        nc.scalar.activation(pt_h(s), bank[4 + s % 2][:, 0:384], ACT.Copy)\
                            .then_inc(pt_hi, 1)
                    if not late:
                        act.wait_ge(masked, L * ITEMS + j + 1)
                        for t, (a, b) in enumerate(((0, P), (P, 3 * P))):
                            q = 2 * (s % 4) + t
                            last = nc.scalar.activation(pr(s)[:, a:b], sc(s)[:, a:b], ACT.Exp,
                                                        bias=nmax[:, q:q + 1], scale=-1.0,
                                                        accum_out=rsum[:, q:q + 1])
                        last.then_inc(exp_done, 1)
                        if s < 4 or not is_(i, PAIRS - 1):
                            proj_high(i, s)
                    if not (is_(i, 0) and s < 3) and not (late and s >= 3):
                        act.wait_ge(ctx_done, L * ITEMS + j - 2)
                        nc.scalar.activation(ctx_slot((s - 3) % 8)[0], bank[6][:, 0:S], ACT.Copy)\
                            .then_inc(ctx_hi, 1)

                for s in range(4, 8):
                    proj_high(-1, s)
                act.wait_ge(v_saved_dve, (L + 1) * 16)
                act.wait_ge(v_saved_act, (L + 1) * 16)

                def pair(i):
                    for s in range(8):
                        step(i, s)
                        if s in (0, 3):
                            v_high(i, s // 3)

                over_pairs(act, pair)
                for s in range(3):
                    step(PAIRS, s, late=True)

                squares(L, False)
                hT_high(3 * L + 1)
                act.wait_ge(lshift, L + 1)
                nc.scalar.activation(prob, prob, ACT.Exp).then_inc(lexp, 1)
                act.wait_ge(cwT_done, L + 1)
                nc.scalar.activation(cwT[:, :], bank[7][0:3 * EROWS, :].bitcast(BF16), ACT.Copy)\
                    .then_inc(cwT_ready, 1)

                def unit(c, hf):
                    m = L * UNITS + 2 * c + hf
                    act.wait_ge(g_done, m + 1)
                    after(act, su_ready, m - 1)
                    nc.scalar.activation(silu_t[hf], bank[4][:, :], ACT.Silu)\
                        .then_inc(silu_ready, 1)
                    act.wait_ge(hw_ready, m + 1)
                    after(act, down_done, m - 1)
                    nc.scalar.activation(hh_h[hf], hw_t[hf], ACT.Copy).then_inc(hh_hi_ready, 1)

                for c in range(3):
                    for hf in range(2):
                        unit(c, hf)
                with act.Fori(1, NCH // 2) as r:
                    for q in range(2):
                        for hf in range(2):
                            unit(2 * r + 1 + q, hf)

                if L == 0:
                    hT_high(2)
                    for u, (c, kind, hf) in enumerate(GU):
                        if kind == 2:
                            continue
                        z = kq_before[u]
                        act.wait_ge(gu_done, u + 1)
                        after(act, gu_phi, z - 3)
                        o = slice(512 * (z % 4), 512 * (z % 4) + 512)
                        nc.scalar.activation(g_e[:, o], bank[4 + u % 4][:, :], ACT.Exp)
                        nc.scalar.activation(g_r[:, o], bank[4 + u % 4][:, :], ACT.Relu)\
                            .then_inc(gu_act, 1)
                    for c in range(DC):
                        act.wait_ge(go_ready, c + 1)
                        nc.scalar.activation(QK[:, 4096 + T * c:4096 + T * c + T],
                                             g_kv[:, T * c:T * c + T], ACT.Copy).then_inc(go_hi, 1)

        @block.vector
        def _(dve):
            v = nc.vector
            steps = [0]

            def link(instruction):
                steps[0] += 1
                instruction.then_inc(dve_step, 1)
                dve.wait_ge(dve_step, steps[0])

            def tile(a, n):
                return a[:, D * n:D * n + D]

            def rsqrt(dst, src, scale, eps):
                link(v.tensor_scalar(rv[:, :], src, scale, eps, ALU.mult, ALU.add))
                link(v.tensor_scalar(ry[:, :].bitcast(I32), rv[:, :].bitcast(I32), -0.5, MAGIC,
                                     ALU.mult, ALU.add))
                for step in range(3):
                    link(v.tensor_tensor(rt[:, :], rv[:, :], ry[:, :], ALU.mult))
                    link(v.scalar_tensor_tensor(rt[:, :], rt[:, :], -0.5, ry[:, :],
                                                ALU.mult, ALU.mult))
                    link(v.scalar_tensor_tensor(dst if step == 2 else ry[:, :], rt[:, :], 1.5,
                                                ry[:, :], ALU.add, ALU.mult))

            stats3 = stats[:, :].rearrange("p (n k) -> p n k", k=6)
            mv3 = mv[:, :].rearrange("p (n k) -> p n k", k=2)

            def layernorm(dst, signal):
                for n in range(NT):
                    last = v.bn_stats(stats3[:, n, :], tile(X, n))
                link(last)
                for n in range(NT):
                    last = v.bn_aggr(mv3[:, n, :], stats3[:, n, :])
                link(last)
                rsqrt(rstd[:, :], mv3[:, :, 1], 1.0, LN_EPS)
                for n in range(NT):
                    v.tensor_scalar(dst[:, D * n:D * n + D], tile(X, n), mv3[:, n, 0:1],
                                    rstd[:, n:n + 1], ALU.subtract, ALU.mult).then_inc(signal, 1)

            def rms_scale(L, first):
                dve.wait_ge(ss_ready, 2 * NT * L + NT * (1 if first else 2))
                rsqrt(rstd[:, :], ss[:, :], 1.0 / D, RMS_EPS)
                for n in range(NT):
                    v.tensor_scalar(Z[:, D * n:D * n + D], tile(Y, n), rstd[:, n:n + 1], None,
                                    ALU.mult).then_inc(z_ready, 1)

            def hT_low(k):
                w = {0: 0, 1: DC, 3: 0, 4: DC}.get(k)
                for q in range(4):
                    hf, c = q // 2, q % 2
                    o = slice(T * c + HALF * hf, T * c + HALF * hf + HALF)
                    dve.wait_ge(hT_hi, 4 * k + q + 1)
                    v.scalar_tensor_tensor(hTl[:, o], bank[q][:, :],
                                           1.0 if w is None else lnw[:, w + c:w + c + 1],
                                           hTh[:, o].bitcast(F32), ALU.mult, ALU.subtract)\
                        .then_inc(hT_ready, 1)

            def gating(L):
                def n16(a): return a.rearrange("p (n e) -> p n e", e=E)
                def per_tile(a): return a.unsqueeze(2).broadcast_to([P, NT, E])
                logits = bank[6][:, 0:NT * E]
                dve.wait_ge(logits_done, L + 1)
                link(v.tensor_reduce(mx8[:, :], n16(logits), X_AXIS, ALU.max))
                v.tensor_tensor(n16(prob), n16(logits), per_tile(mx8[:, :]), ALU.subtract)\
                    .then_inc(lshift, 1)
                dve.wait_ge(lexp, L + 1)
                link(v.tensor_reduce(sm8[:, :], n16(prob), X_AXIS, ALU.add))
                link(v.reciprocal(rs8[:, :], sm8[:, :]))
                link(v.tensor_tensor(n16(prob), n16(prob), per_tile(rs8[:, :]), ALU.mult))
                for n in range(NT):
                    last = v.max(top8[:, 8 * n:8 * n + 8], prob[:, E * n:E * n + E])
                link(last)
                least = top8[:, :].rearrange("p (n k) -> p n k", k=8)[:, :, TOPK - 1:TOPK]\
                    .broadcast_to([P, NT, E])
                v.tensor_tensor(n16(gt_t), n16(prob), least, ALU.is_gt)
                link(v.tensor_tensor(n16(eq_t), n16(prob), least, ALU.is_equal))
                v.tensor_reduce(cg8[:, :], n16(gt_t), X_AXIS, ALU.add)
                link(v.tensor_tensor_scan(inc_t, seg[:, :], eq_t, 0.0, ALU.mult, ALU.add))
                link(v.tensor_tensor(n16(inc_t), n16(inc_t), per_tile(cg8[:, :]), ALU.add))
                link(v.scalar_tensor_tensor(sel_t, inc_t, float(TOPK), eq_t, ALU.is_le, ALU.mult))
                link(v.tensor_tensor(sel_t, sel_t, gt_t, ALU.add))
                link(v.tensor_tensor(prob, prob, sel_t, ALU.mult))
                link(v.tensor_reduce(sm8[:, :], n16(prob), X_AXIS, ALU.add))
                link(v.reciprocal(rs8[:, :], sm8[:, :]))
                cwv = cw[:, :].rearrange("p (n e) -> p n e", e=EROWS)
                v.memset(cwv[:, :, E:E + SI // I], 1.0)
                v.memset(cwv[:, :, E + SI // I:EROWS], 0.0)
                link(v.tensor_tensor(cwv[:, :, 0:E], n16(prob), per_tile(rs8[:, :]), ALU.mult))
                part = cw3[:, :].rearrange("p (n a e) -> p n a e", a=3, e=EROWS)
                r1, r2 = (a.rearrange("p (n e) -> p n e", e=EROWS) for a in (rest1, rest2))
                link(v.tensor_copy(part[:, :, 0, :], cwv))
                link(v.tensor_tensor(r1, cwv, part[:, :, 0, :], ALU.subtract))
                link(v.tensor_copy(part[:, :, 1, :], r1))
                link(v.tensor_tensor(r2, r1, part[:, :, 1, :], ALU.subtract))
                v.tensor_copy(part[:, :, 2, :], r2).then_inc(cw3_ready, 1)

            dve.wait_ge(ld_const, 16 * 6)
            for L in range(2):
                if L == 0:
                    for n in range(2):
                        dve.wait_ge(ld_x[n], 16)
                else:
                    dve.wait_ge(gout_added, 4)
                    dve.wait_ge(x_half, 1)
                layernorm(Y, y_ready)
                rms_scale(L, True)
                hT_low(3 * L)

                def v_block(cb):
                    for n in range(1, NT, 2):
                        dve.wait_ge(v_done, L * 4 * NT + 8 * cb + n + 1)
                        v.tensor_copy(v3[:, n, bass.ds(512 * cb, 512)], bank[4 + n % 4][:, :])\
                            .then_inc(v_saved_dve, 1)
                with dve.Fori(0, 4) as cb:
                    v_block(cb)

                def proj_low(i, s):
                    dve.wait_ge(proj_hi, L * ITEMS + 8 * i + 4 + s + 1)
                    slot, o = (0 if s >= 4 else 1), HALF * ((s % 4) // 2)
                    high, low = ((q_h, q_l), (k_h, k_l))[s % 2]
                    v.tensor_tensor(low(slot)[:, o:o + HALF], bank[s % 2][:, :],
                                    high(slot)[:, o:o + HALF].bitcast(F32), ALU.subtract)\
                        .then_inc(proj_ready, 1)

                def step(i, s, late=False):
                    j = 8 * i + s
                    if not (is_(i, 0) and s < 1) and not (late and s >= 1):
                        q = 2 * ((s - 1) % 4)
                        dve.wait_ge(exp_done, L * ITEMS + j)
                        v.reciprocal(rinv[:, q:q + 2], rsum[:, q:q + 2]).then_inc(rinv_ready, 1)
                    if not late:
                        after_alone(dve, scores_done, L * ITEMS + j + 1, dve_passed)
                        for t, (a, b) in enumerate(((0, P), (P, 3 * P))):
                            q = 2 * (s % 4) + t
                            last = v.tensor_tensor_reduce(
                                out=sc(s)[:, a:b], in0=bank[2 + s % 2][:, a:b], in1=mask[:, a:b],
                                scale=-SCALE, scalar=3.0e38, op0=ALU.add, op1=ALU.min,
                                accum_out=nmax[:, q:q + 1])
                        last.then_inc(masked, 1)
                    if not (is_(i, 0) and s < 2) and not (late and s >= 2):
                        dve.wait_ge(pt_hi, L * ITEMS + j - 1)
                        v.tensor_tensor(pt_l(s), bank[4 + s % 2][:, 0:384], pt_h(s).bitcast(F32),
                                        ALU.subtract).then_inc(pt_ready, 1)
                    if not late and (s < 4 or not is_(i, PAIRS - 1)):
                        proj_low(i, s)
                    if not (is_(i, 0) and s < 3) and not (late and s >= 3):
                        high, low = ctx_slot((s - 3) % 8)
                        dve.wait_ge(ctx_hi, L * ITEMS + j - 2)
                        v.tensor_tensor(low, bank[6][:, 0:S], high.bitcast(F32), ALU.subtract)\
                            .then_inc(ctx_ready, 1)
                    if s < 4 and not is_(i, 0):
                        dve.wait_ge(wo_done, L * 4 * PAIRS + 4 * (i - 1) + s + 1)
                        y2 = Y[:, 512 * s:512 * s + 512]
                        v.tensor_tensor(y2, bank[7][:, :], y2, ALU.add).then_inc(wo_added, 1)

                for s in range(4, 8):
                    proj_low(-1, s)

                def pair(i):
                    for s in range(8):
                        step(i, s)

                over_pairs(dve, pair)
                for s in range(4):
                    step(PAIRS, s, late=True)

                dve.wait_ge(wo_added, (L + 1) * 4 * PAIRS)
                rms_scale(L, False)
                hT_low(3 * L + 1)
                gating(L)

                def unit(c, hf):
                    m = L * UNITS + 2 * c + hf
                    dve.wait_ge(silu_ready, m + 1)
                    dve.wait_ge(u_done, m + 1)
                    v.tensor_tensor(su_t, bank[5][:, :], silu_t[hf], ALU.mult)\
                        .then_inc(su_ready, 1)
                    dve.wait_ge(su_ready, m + 1)
                    dve.wait_ge(cwb_done, m + 1)
                    v.tensor_tensor(hw_t[hf], bank[6][:, :], su_t, ALU.mult).then_inc(hw_ready, 1)
                    dve.wait_ge(hh_hi_ready, m + 1)
                    v.tensor_tensor(hh_l[hf], hw_t[hf], hh_h[hf].bitcast(F32), ALU.subtract)\
                        .then_inc(hh_ready, 1)

                for c in range(3):
                    for hf in range(2):
                        unit(c, hf)
                with dve.Fori(1, NCH // 2) as r:
                    for q in range(2):
                        for hf in range(2):
                            unit(2 * r + 1 + q, hf)
                dve.wait_ge(x_half, L + 1)
                dve.wait_ge(down_done, (L + 1) * UNITS)
                for q in range(4):
                    x2 = X[:, 512 * q:512 * q + 512]
                    v.scalar_tensor_tensor(x2, bank[q][:, :], 0.5, x2, ALU.mult, ALU.add)\
                        .then_inc(x_moe, 1)

                if L == 0:
                    dve.wait_ge(x_moe, 4)
                    layernorm(Z, z_ready)
                    hT_low(2)
                    for u, (c, kind, hf) in enumerate(GU):
                        o = slice(T * c + HALF * hf, T * c + HALF * hf + HALF)
                        if kind < 2:
                            z = kq_before[u]
                            e = slice(512 * (z % 4), 512 * (z % 4) + 512)
                            dve.wait_ge(gu_act, z + 1)
                            v.scalar_tensor_tensor((g_k, g_q)[kind][:, o], g_e[:, e], 1.0,
                                                   g_r[:, e], ALU.min, ALU.add).then_inc(gu_phi, 1)
                            continue
                        dve.wait_ge(gu_done, u + 1)
                        dve.wait_ge(gu_phi, kq_before[u])
                        v.tensor_tensor(g_kv[:, o], bank[4 + u % 4][:, :], g_k[:, o], ALU.mult)\
                            .then_inc(gu_kv, 1)
                        if hf == 0:
                            continue
                        dve.wait_ge(gu_kv, v_before[u] + 1)
                        for b in range(NB):
                            w = slice(T * c + S * b, T * c + S * b + S)
                            v.tensor_tensor_scan(g_kvc[:, w], g_kv[:, w], g_kv[:, w], 0.0,
                                                 ALU.add, ALU.bypass)
                            last = v.tensor_tensor_scan(g_kc[:, w], g_k[:, w], g_k[:, w], 0.0,
                                                        ALU.add, ALU.bypass)
                        link(last)
                        w = slice(T * c, T * c + T)
                        v.tensor_tensor(g_kv[:, w], g_q[:, w], g_kvc[:, w], ALU.mult)
                        link(v.tensor_tensor(g_k[:, w], g_q[:, w], g_kc[:, w], ALU.mult))
                        link(v.tensor_scalar(g_k[:, w], g_k[:, w], GLA_EPS, None, ALU.add))
                        link(v.reciprocal(g_kc[:, w], g_k[:, w]))
                        v.tensor_tensor(g_kv[:, w], g_kv[:, w], g_kc[:, w], ALU.mult)\
                            .then_inc(go_ready, 1)
                    for c in range(DC):
                        w = slice(T * c, T * c + T)
                        dve.wait_ge(go_hi, c + 1)
                        v.tensor_tensor(QK[:, 6144 + T * c:6144 + T * c + T], g_kv[:, w],
                                        QK[:, 4096 + T * c:4096 + T * c + T].bitcast(F32),
                                        ALU.subtract).then_inc(go_lo, 1)
                    for q in range(4):
                        dve.wait_ge(gout_done, q + 1)
                        x2 = X[:, 512 * q:512 * q + 512]
                        v.scalar_tensor_tensor(x2, bank[q][:, :], GLA_SCALE, x2, ALU.mult, ALU.add)\
                            .then_inc(gout_added, 1)

        @block.tensor
        def _(pe):
            def product(o, terms, start=True, stop=True):
                passes = [(a, b) for sh, sl, mh, ml in terms for a, b in ((sl, mh), (sh, ml), (sh, mh))]
                for n, (a, b) in enumerate(passes):
                    last = nc.tensor.matmul(o, a, b, start=start and n == 0,
                                            stop=stop and n == len(passes) - 1,
                                            skip_group_check=not (start and stop))
                return last

            def hT(c, a, n):
                return hTh[:, T * c + a:T * c + a + n], hTl[:, T * c + a:T * c + a + n]

            def transpose_z(k):
                for q in range(4):
                    hf, c = q // 2, q % 2
                    for n in range(4):
                        t = 4 * hf + n
                        if c == 0:
                            pe.wait_ge(z_ready, NT * k + t + 1)
                        last = nc.tensor.transpose(bank[q][:, P * n:P * n + P],
                                                   Z[:, D * t + P * c:D * t + P * c + P], ident[:, :])
                    last.then_inc(zT_done, 1)

            pe.wait_ge(ld_const, 16 * 6)
            for L in range(2):
                transpose_z(3 * L)

                def v_block(cb):
                    pe.wait_ge(wv_ready, 4 * L + cb + 1)
                    for n in range(NT):
                        if is_(cb, 0) and n in (0, 4):
                            pe.wait_ge(hT_ready, 4 * 3 * L + (2 if n == 0 else 4))
                        if not is_(cb, 0) or n >= 4:
                            pe.wait_ge((v_saved_act, v_saved_dve)[n % 2],
                                       L * 16 + 4 * cb + n // 2 - 1)
                        product(bank[4 + n % 4][:, :],
                                [(*hT(c, P * n, P),
                                  QK[:, bass.ds(2048 * cb + 512 * c, 512)],
                                  QK[:, bass.ds(2048 * cb + 1024 + 512 * c, 512)])
                                 for c in range(DC)]).then_inc(v_done, 1)
                v_block(0)
                with pe.Fori(1, 4) as cb:
                    v_block(cb)

                def proj(i, s):
                    k = L * ITEMS + 8 * i + 4 + s
                    slot, qk, hf = (0 if s >= 4 else 1), s % 2, (s % 4) // 2
                    if s % 4 == 0:
                        pe.wait_ge(wqk_ready, L * H + 2 * i + s // 4 + 2)
                    after(pe, proj_ready, k - 1)
                    product(bank[s % 2][:, :],
                            [(*ring(slot, D * qk + P * c, P), *hT(c, HALF * hf, HALF))
                             for c in range(DC)]).then_inc(proj_done, 1)

                for s in range(4, 8):
                    proj(-1, s)
                pe.wait_ge(v_saved_act, (L + 1) * 16)
                pe.wait_ge(v_saved_dve, (L + 1) * 16)

                def step(i, s, late=False):
                    j = 8 * i + s
                    if not late:
                        slot, b = s // 4, s % 4
                        if b in (0, 2):
                            pe.wait_ge(proj_ready, L * ITEMS + 8 * i + 4 * slot + b + 2)
                        after(pe, masked, L * ITEMS + j - 1)
                        o = bank[2 + s % 2]
                        for a, w, t in ((0, P, 0), (P, 2 * P, 1)):
                            q0, k0 = S * b + P * t, S * b
                            last = product(o[:, a:a + w],
                                           [(q_h(slot)[:, q0:q0 + P], q_l(slot)[:, q0:q0 + P],
                                             k_h(slot)[:, k0:k0 + w], k_l(slot)[:, k0:k0 + w])])
                        last.then_inc(scores_done, 1)
                    if not (is_(i, 0) and s < 2) and not (late and s >= 2):
                        pe.wait_ge(probs_ready, L * ITEMS + j - 1)
                        after(pe, pt_ready, L * ITEMS + j - 3)
                        for n in range(3):
                            last = nc.tensor.transpose(bank[4 + s % 2][:, P * n:P * n + P],
                                                       pr(s - 2)[:, P * n:P * n + P], ident[:, :])
                        last.then_inc(probsT_done, 1)
                    if not late and (s < 4 or not is_(i, PAIRS - 1)):
                        proj(i, s)
                    if not (is_(i, 0) and s < 3) and not (late and s >= 3):
                        t = (s - 3) % 8
                        slot, b = t // 4, t % 4
                        if b == 0:
                            pe.wait_ge(vs_ready, L * H + 2 * (i - (1 if s < 3 else 0)) + slot + 1)
                        pe.wait_ge(pt_ready, L * ITEMS + j - 2)
                        after(pe, ctx_ready, L * ITEMS + j - 3)
                        def vt(n): return (v_h(slot)[:, P * n:P * n + P], v_l(slot)[:, P * n:P * n + P])
                        ph, pl = pt_h(t), pt_l(t)
                        product(bank[6][:, 0:S], [(*vt(2 * b), ph[:, 0:S], pl[:, 0:S])], stop=False)
                        product(bank[6][:, P:S], [(*vt(2 * b + 1), ph[:, S:384], pl[:, S:384])],
                                start=False).then_inc(ctx_done, 1)
                    if s < 4 and not is_(i, 0):
                        w = L * 4 * PAIRS + 4 * (i - 1) + s
                        if s == 0:
                            pe.wait_ge(wo_ready, L * H + 2 * i)
                        pe.wait_ge(ctx_ready, L * ITEMS + 8 * (i - 1) + 4 + s + 1)
                        after(pe, wo_added, w)
                        for t in range(2):
                            def part(g):
                                hi, lo = ctx_slot(4 * g + s)
                                return hi[:, P * t:P * t + P], lo[:, P * t:P * t + P]
                            last = product(bank[7][:, D * t:D * t + D],
                                           [(*part(g), *ring(g, QKW, WOW)) for g in range(2)])
                        last.then_inc(wo_done, 1)

                def pair(i):
                    for s in range(8):
                        step(i, s)

                over_pairs(pe, pair)
                for s in range(4):
                    step(PAIRS, s, late=True)

                transpose_z(3 * L + 1)
                pe.wait_ge(hT_ready, 4 * (3 * L + 2))
                pe.wait_ge(gw_ready, 1)
                for n in range(NT):
                    last = product(bank[6][:, E * n:E * n + E],
                                   [(*hT(c, P * n, P), gwh[:, E * c:E * c + E], gwl[:, E * c:E * c + E])
                                    for c in range(DC)])
                last.then_inc(logits_done, 1)

                def combine_transposes():
                    pe.wait_ge(cw3_ready, L + 1)
                    o = bank[7][0:3 * EROWS, :].bitcast(BF16)
                    for n in range(NT):
                        last = nc.tensor.transpose(o[:, P * n:P * n + P],
                                                   cw3[:, 3 * EROWS * n:3 * EROWS * n + 3 * EROWS],
                                                   identb[:, :])
                    last.then_inc(cwT_done, 1)
                    pe.wait_ge(cwT_ready, L + 1)

                def down(c, s, hf, first):
                    m = L * UNITS + 2 * c + hf
                    if hf == 0:
                        pe.wait_ge(moe_ready, 2 * (L * NCH + c) + 2)
                    pe.wait_ge(hh_ready, m + 1)
                    for t in range(4):
                        last = product(bank[2 * hf + t // 2][:, D * (t % 2):D * (t % 2) + D],
                                       [(hh_h[hf][:, P * t:P * t + P], hh_l[hf][:, P * t:P * t + P],
                                         *ring(s, 2 * D, D))], start=first and t % 2 == 0, stop=False)
                    last.then_inc(down_done, 1)

                def unit(c, s, hf):
                    m = L * UNITS + 2 * c + hf
                    if hf == 0:
                        pe.wait_ge(moe_ready, 2 * (L * NCH + c) + 1)
                    after(pe, silu_ready, m)
                    product(bank[4][:, :], [(*ring(s, P * d, P), *hT(d, HALF * hf, HALF))
                                            for d in range(DC)]).then_inc(g_done, 1)
                    after(pe, su_ready, m)
                    product(bank[5][:, :], [(*ring(s, D + P * d, P), *hT(d, HALF * hf, HALF))
                                            for d in range(DC)]).then_inc(u_done, 1)
                    if is_(c, 0) and hf == 0:
                        combine_transposes()
                    after(pe, hw_ready, m)
                    nc.tensor.matmul(bank[6][:, :], sel[:, bass.ds(P * c, P)],
                                     cwT[:, HALF * hf:HALF * hf + HALF], start=True, stop=True)\
                        .then_inc(cwb_done, 1)
                    if hf:
                        down(c, s, 0, is_(c, 0))
                    elif not is_(c, 0):
                        down(c - 1, 1 - s, 1, is_(c, 1))

                if L == 0:
                    pe.wait_ge(ld_sel, 16)
                for c in range(3):
                    for hf in range(2):
                        unit(c, c % 2, hf)
                with pe.Fori(1, NCH // 2) as r:
                    for q in range(2):
                        for hf in range(2):
                            unit(2 * r + 1 + q, 1 - q, hf)
                down(NCH - 1, 0, 1, False)

                if L == 0:
                    transpose_z(2)
                    pe.wait_ge(gla_w_ready, 1)
                    for u, (c, kind, hf) in enumerate(GU):
                        if u in (0, 1):
                            pe.wait_ge(hT_ready, 4 * 2 + 2 * (hf + 1))
                        if u >= 4:
                            w = u - 4
                            if GU[w][1] < 2:
                                pe.wait_ge(gu_act, kq_before[w] + 1)
                            else:
                                pe.wait_ge(gu_kv, v_before[w] + 1)
                        col = (D, 0, 2 * D)[kind] + P * c
                        product(bank[4 + u % 4][:, :],
                                [(QK[:, 768 * d + col:768 * d + col + P],
                                  QK[:, 1536 + 768 * d + col:1536 + 768 * d + col + P],
                                  *hT(d, HALF * hf, HALF)) for d in range(DC)]).then_inc(gu_done, 1)
                    pe.wait_ge(gla_w_ready, 2)
                    pe.wait_ge(go_lo, DC)
                    for q in range(4):
                        for t in range(2):
                            a = P * (2 * q + t)
                            last = product(bank[q][:, D * t:D * t + D],
                                           [(QK[:, 4096 + T * c + a:4096 + T * c + a + P],
                                             QK[:, 6144 + T * c + a:6144 + T * c + a + P],
                                             QK[:, 3072 + D * c:3072 + D * c + D],
                                             QK[:, 3584 + D * c:3584 + D * c + D])
                                            for c in range(DC)])
                        last.then_inc(gout_done, 1)


def kernel(**inputs):
    import concourse.bacc as bacc
    import ml_dtypes
    from concourse.bass_utils import run_bass_kernel_spmd

    a = {n.removeprefix("L0_").removeprefix("ffn_").removeprefix("attn_"): np.asarray(v)
         for n, v in inputs.items()}

    def by_partition(w, axis_first=True):
        return np.ascontiguousarray(w.reshape(-1, P, w.shape[-1]).transpose(1, 0, 2))

    def per_head(w):
        return w.reshape(DC, P, H, HD).transpose(2, 1, 0, 3).reshape(H, P, DC * HD)

    def per_chunk(w):
        w = np.pad(w, ((0, NCH * P - UP), (0, 0)))
        return w.reshape(NCH, P, DC, P).transpose(0, 3, 2, 1).reshape(NCH, P, DC * P)

    gate = np.concatenate([a["eg_w"].reshape(E * I, D), a["sg_w"]])
    up = np.concatenate([a["eu_w"].reshape(E * I, D), a["su_w"]])
    down = np.concatenate([a["ed_w"].transpose(0, 2, 1).reshape(E * I, D), a["sd_w"].T])
    down = np.pad(down, ((0, NCH * P - UP), (0, 0))).reshape(NCH, P, D)

    causal = np.where(np.tri(P, dtype=bool), 0.0, -1e30).astype(np.float32)
    mask = np.concatenate([causal, np.zeros((P, P), np.float32), causal], 1)
    seg = np.tile((np.arange(E * NT) % E != 0).astype(np.float32), (P, 1))
    sel = (np.arange(NCH * P)[None, :] // I == np.arange(3 * EROWS)[:, None] % EROWS)
    arrays = {
        "x": a["x"].reshape(NT, P, D).transpose(1, 0, 2),
        "wqk": np.concatenate([per_head(a["wq"]), per_head(a["wk"])], 2),
        "wo": a["wo"].reshape(H, HD, D),
        "wv": by_partition(a["wv"]),
        "moe": np.concatenate([per_chunk(gate), per_chunk(up), down], 2),
        "gate": by_partition(a["gate_w"].T).reshape(P, DC * E),
        "ln": np.concatenate([a["ln1_w"].reshape(DC, P).T, a["ln2_w"].reshape(DC, P).T], 1),
        "wqkv": by_partition(a["W_qkv"].T).reshape(P, DC * 3 * D),
        "wout": by_partition(a["W_out"].T).reshape(P, DC * D),
        "ident": np.eye(P, dtype=np.float32),
        "identb": np.eye(P, dtype=ml_dtypes.bfloat16),
        "mask": mask,
        "seg": seg,
        "sel": sel.astype(ml_dtypes.bfloat16),
    }
    arrays = {n + "_dram": np.ascontiguousarray(v) for n, v in arrays.items()}
    nc = bacc.Bacc("TRN2", target_bir_lowering=False, num_devices=1)
    args = [nc.dram_tensor(n, v.shape, mybir.dt.from_np(v.dtype), kind="ExternalInput").ap()
            for n, v in arrays.items()]
    out = nc.dram_tensor("out_dram", (P, NT, D), F32, kind="ExternalOutput").ap()
    program(nc, *args, out)
    r = run_bass_kernel_spmd(nc, [arrays], core_ids=[0])
    y = r.results[0]["out_dram"]
    return np.ascontiguousarray(y.transpose(1, 0, 2)).reshape(NB, S, D)
```

```python
import numpy as np
import concourse.bass as bass
from concourse import mybir
from contextlib import ExitStack

F32 = mybir.dt.float32
F32R = mybir.dt.float32r
BF16 = mybir.dt.bfloat16
I32 = mybir.dt.int32
ALU = mybir.AluOpType
ACT = mybir.ActivationFunctionType
X_AXIS = mybir.AxisListType.X

P = 128
T, D = 1024, 256
NT, DC = T // P, D // P
NB, S = 4, 256
H, HD = 16, 128
PAIRS = H // 2
E, I, SI, TOPK = 16, 176, 352, 6
EROWS = 32
UP = E * I + SI
NCH = -(-UP // P)
HALF = 512
SCALE = float(HD) ** -0.5
GLA_SCALE = float(D // 16) ** -0.5
LN_EPS, RMS_EPS, GLA_EPS = 1e-5, 1e-6, 1e-9
QKW, WOW = 2 * D, D
MW = 3 * D
ITEMS = H * NB
UNITS = 2 * NCH
LATE_WO = (7, 2, 3, 7)
TL, CL, WL = 3, 4, 5
MAGIC = 1597463007.0


def program(nc, x_in, wqk_in, wo_in, wv_in, moe_in, gate_in, ln_in, wqkv_in, wout_in,
            ident_in, identb_in, mask_in, seg_in, sel_in, out):
    ctx = ExitStack()
    with ctx:
        def sb(name, cols, dt, parts=P):
            return ctx.enter_context(nc.sbuf_tensor(name, [parts, cols], dt))

        def sem(name):
            return ctx.enter_context(nc.semaphore(name))

        X = sb("X", NT * D, F32)
        Y = sb("Y", NT * D, F32)
        big = sb("big", NT * H * HD, F32)
        Z = big[:, 0:NT * D]
        silu_t = [big[:, 2048 + 512 * s:2560 + 512 * s] for s in range(2)]
        su_t = [big[:, 9216 + 512 * s:9728 + 512 * s] for s in range(4)]
        hw_t = [big[:, 3584 + 512 * s:4096 + 512 * s] for s in range(2)]
        prob = big[:, 4608:4736]
        gt_t, eq_t, inc_t, sel_t = (big[:, 4736 + 128 * s:4864 + 128 * s] for s in range(4))
        rest1 = big[:, 5248:5504]
        rest2 = big[:, 5504:5760]
        cw = big[:, 5760:6016]
        cw3 = big[:, 6016:6400].bitcast(BF16)
        cwT = big[0:3 * EROWS, 6400:6912].bitcast(BF16)
        squared = big[:, 7168:9216]
        lgT = big[0:E, 11264:12288]
        g_e, g_r = big[:, 2048:4096], big[:, 4096:6144]
        g_k, g_q, g_kv = big[:, 6144:8192], big[:, 8192:10240], big[:, 10240:12288]
        g_kc, g_kvc = big[:, 12288:14336], big[:, 14336:16384]
        v3 = big[:, :].rearrange("p (n f) -> p n f", n=NT)

        hTh, hTl = sb("hTh", DC * T, F32R), sb("hTl", DC * T, F32R)
        Wh, Wl = sb("Wh", 2 * MW, F32R), sb("Wl", 2 * MW, F32R)
        QK = sb("QK", 8 * T, F32R)
        Vs = sb("Vs", 4 * T, F32R)
        PT = sb("PT", 4 * 384, F32R)
        CA = sb("CA", 2 * T, F32R)
        CB = sb("CB", 4 * S, F32R)
        SP_ = sb("SP_", 6 * 384, F32)
        raw_qk, raw_wo = sb("raw_qk", 2 * QKW, F32), sb("raw_wo", 2 * WOW, F32)
        raw_moe = sb("raw_moe", 2 * MW, F32)
        ident, identb = sb("ident", P, F32), sb("identb", P, BF16)
        mask, seg = sb("mask", 384, F32), sb("seg", P, F32)
        sel = sb("sel", NCH * P, BF16, 3 * EROWS)
        lnw = sb("lnw", 2 * DC, F32)
        graw = sb("graw", DC * E, F32)
        gwh, gwl = sb("gwh", DC * E, F32R), sb("gwl", DC * E, F32R)
        stats, mv = sb("stats", NT * 6, F32), sb("mv", NT * 2, F32)
        ss = sb("ss", NT, F32)
        rstd, rms, ms, rv, ry, rt = (sb(n, NT, F32) for n in ("rstd", "rms", "ms", "rv", "ry", "rt"))
        nmax, rsum, rinv = (sb(n, 8, F32) for n in ("nmax", "rsum", "rinv"))
        mx8, sm8, rs8, cg8 = (sb(n, NT, F32) for n in ("mx8", "sm8", "rs8", "cg8"))
        top8 = sb("top8", NT * 8, F32)

        bank = [ctx.enter_context(nc.psum_tensor(f"bank{i}", [P, 512], F32)) for i in range(8)]

        def q_h(s): return QK[:, 4096 * s:4096 * s + 1024]
        def q_l(s): return QK[:, 4096 * s + 1024:4096 * s + 2048]
        def k_h(s): return QK[:, 4096 * s + 2048:4096 * s + 3072]
        def k_l(s): return QK[:, 4096 * s + 3072:4096 * s + 4096]
        def v_h(s): return Vs[:, 2048 * s:2048 * s + 1024]
        def v_l(s): return Vs[:, 2048 * s + 1024:2048 * s + 2048]
        def sc(j): return SP_[:, 384 * (j % 2):384 * (j % 2) + 384]
        def pr(j): return SP_[:, 384 * (2 + j % 4):384 * (2 + j % 4) + 384]
        def pt_h(j): return PT[:, 768 * (j % 2):768 * (j % 2) + 384]
        def pt_l(j): return PT[:, 768 * (j % 2) + 384:768 * (j % 2) + 768]
        def ring(s, a, n): return Wh[:, MW * s + a:MW * s + a + n], Wl[:, MW * s + a:MW * s + a + n]
        hh_h = [CA[:, 1024 * s:1024 * s + 512] for s in range(2)]
        hh_l = [CA[:, 1024 * s + 512:1024 * s + 1024] for s in range(2)]

        def ctx_slot(s):
            if s < 4:
                return CA[:, S * s:S * s + S], CA[:, 1024 + S * s:1024 + S * s + S]
            c = 2 * S * (s % 2)
            return CB[:, c:c + S], CB[:, c + S:c + 2 * S]

        ld_x = [sem(f"ld_x{n}") for n in range(2)]
        ld_const, ld_sel = sem("ld_const"), sem("ld_sel")
        ld_wv = [sem(f"ld_wv{s}") for s in range(2)]
        ld_qk = [sem(f"ld_qk{s}") for s in range(2)]
        ld_wo = [sem(f"ld_wo{s}") for s in range(2)]
        ld_moe = [sem(f"ld_moe{s}") for s in range(2)]
        ld_gqkv, ld_gout = sem("ld_gqkv"), sem("ld_gout")
        stored = sem("stored")
        pool_passed, dve_passed = sem("pool_passed"), sem("dve_passed")
        dve_step = sem("dve_step")
        y_ready, ss_ready, z_ready = sem("y_ready"), sem("ss_ready"), sem("z_ready")
        zT_done, hT_hi, hT_ready = sem("zT_done"), sem("hT_hi"), sem("hT_ready")
        wv_hi, wv_ready = sem("wv_hi"), sem("wv_ready")
        wqk_hi, wqk_ready = sem("wqk_hi"), sem("wqk_ready")
        wo_hi, wo_ready = sem("wo_hi"), sem("wo_ready")
        moe_hi, gu_w_ready, down_w_ready = sem("moe_hi"), sem("gu_w_ready"), sem("down_w_ready")
        gw_hi, gw_ready = sem("gw_hi"), sem("gw_ready")
        gla_hi, gla_w_ready = sem("gla_hi"), sem("gla_w_ready")
        v_done, v_saved_act, v_saved_dve = sem("v_done"), sem("v_saved_act"), sem("v_saved_dve")
        vs_hi, vs_ready = sem("vs_hi"), sem("vs_ready")
        proj_done, proj_hi, proj_ready = sem("proj_done"), sem("proj_hi"), sem("proj_ready")
        scores_done, masked = sem("scores_done"), sem("masked")
        exp_done, rinv_ready, probs_ready = sem("exp_done"), sem("rinv_ready"), sem("probs_ready")
        probsT_done, pt_hi, pt_ready = sem("probsT_done"), sem("pt_hi"), sem("pt_ready")
        ctx_done, ctx_hi, ctx_ready = sem("ctx_done"), sem("ctx_hi"), sem("ctx_ready")
        wo_done, wo_added = sem("wo_done"), sem("wo_added")
        lgT_done, lgT_ready = sem("lgT_done"), sem("lgT_ready")
        logits_done, lshift, lexp = sem("logits_done"), sem("lshift"), sem("lexp")
        cw3_ready, cwT_done, cwT_ready = sem("cw3_ready"), sem("cwT_done"), sem("cwT_ready")
        y_halved, x_half = sem("y_halved"), sem("x_half")
        g_done, silu_ready, u_done, su_ready = (
            sem("g_done"), sem("silu_ready"), sem("u_done"), sem("su_ready"))
        cwb_done, hw_ready, hh_hi_ready, hh_ready = (
            sem("cwb_done"), sem("hw_ready"), sem("hh_hi_ready"), sem("hh_ready"))
        down_done, x_moe = sem("down_done"), sem("x_moe")
        gu_done, gu_act, gu_phi, gu_kv = sem("gu_done"), sem("gu_act"), sem("gu_phi"), sem("gu_kv")
        go_ready, go_hi, go_lo = sem("go_ready"), sem("go_hi"), sem("go_lo")
        gout_done, gout_added = sem("gout_done"), sem("gout_added")
        block = ctx.enter_context(nc.Block())


        def after(eng, sm, value):
            if not isinstance(value, int) or value > 0:
                eng.wait_ge(sm, value)

        def after_alone(eng, sm, value, passed):
            if not isinstance(value, int) or value > 0:
                eng.wait_ge(sm, value)
                eng.sem_inc(passed, 1)

        def over_pairs(eng, body):
            body(0)
            with eng.Fori(1, PAIRS - 1) as i:
                body(i)
            body(PAIRS - 1)

        def is_(i, value):
            return isinstance(i, int) and i == value

        def up_bank(c, hf):
            return {(0, 1): 2, (1, 0): 3}.get((c, hf), 5) if isinstance(c, int) else 5

        def cwT_bank(hf):
            return bank[(6, 2)[hf]][0:3 * EROWS, 0:HALF // 2].bitcast(BF16)

        GU = [(u // 6, (u % 6) // 2, u % 2) for u in range(12)]
        kq_before = [sum(GU[w][1] < 2 for w in range(u)) for u in range(13)]
        v_before = [u - kq_before[u] for u in range(13)]

        @block.sync
        def _(sp):
            for n in range(2):
                sp.dma_start(X[:, 1024 * n:1024 * n + 1024].rearrange("p (n d) -> p n d", n=4),
                             x_in[:, 4 * n:4 * n + 4, :]).then_inc(ld_x[n], 16)
            for dst, src in ((ident, ident_in), (lnw, ln_in), (graw, gate_in), (identb, identb_in),
                             (mask, mask_in), (seg, seg_in)):
                sp.dma_start(dst[:, :], src).then_inc(ld_const, 16)

            def head(src, g):
                return src[bass.ds(g, 1), :, :].rearrange("a p f -> (a p) f")

            def qk(L, i, s):
                after(sp, wqk_ready, L * H + 2 * (i - 1) + s + 1)
                sp.dma_start(raw_qk[:, QKW * s:QKW * s + QKW], head(wqk_in, 2 * i + s))\
                    .then_inc(ld_qk[s], 16)

            def wo(L, i, s):
                after(sp, wo_ready, L * H + 2 * (i - 1) + s + 1)
                sp.dma_start(raw_wo[:, WOW * s:WOW * s + WOW], head(wo_in, 2 * i + s))\
                    .then_inc(ld_wo[s], 16)

            def chunk(L, c, s):
                after(sp, down_w_ready, L * NCH + c - 1)
                sp.dma_start(raw_moe[:, MW * s:MW * s + MW], head(moe_in, c))\
                    .then_inc(ld_moe[s], 16)

            for L in range(2):
                if L:
                    sp.wait_ge(probsT_done, ITEMS)
                for cb in range(4):
                    if cb >= 2:
                        sp.wait_ge(wv_ready, 4 * L + cb - 1)
                    s = cb % 2
                    sp.dma_start(SP_[:, 1024 * s:1024 * s + 1024].rearrange("p (c f) -> p c f", c=DC),
                                 wv_in[:, :, 512 * cb:512 * cb + 512]).then_inc(ld_wv[s], 16)
                    if cb == 1:
                        qk(L, 0, 0)
                        qk(L, 0, 1)
                if L == 0:
                    sp.dma_start(sel[:, :], sel_in).then_inc(ld_sel, 16)
                else:
                    sp.wait_ge(gla_w_ready, 2)

                def pair(i):
                    for s in range(2):
                        wo(L, i, s)
                    if not is_(i, PAIRS - 1):
                        for s in range(2):
                            qk(L, i + 1, s)

                over_pairs(sp, pair)
                if L:
                    sp.wait_ge(gla_w_ready, 1)
                for c in range(3):
                    chunk(L, c, c % 2)
                with sp.Fori(1, NCH // 2) as r:
                    chunk(L, 2 * r + 1, 1)
                    chunk(L, 2 * r + 2, 0)
                if L == 0:
                    sp.wait_ge(wo_ready, H)
                    sp.dma_start(raw_wo[:, :], wout_in).then_inc(ld_gout, 16)
                    sp.wait_ge(down_w_ready, NCH)
                    sp.dma_start(raw_moe[:, :], wqkv_in).then_inc(ld_gqkv, 16)
            for q in range(4):
                sp.wait_ge(x_moe, 4 + q + 1)
                sp.dma_start(out[:, 2 * q:2 * q + 2, :],
                             X[:, 512 * q:512 * q + 512].rearrange("p (n d) -> p n d", n=2))\
                    .then_inc(stored, 16)
            sp.wait_ge(stored, 16 * 4)

        @block.gpsimd
        def _(pool):
            def split(hi, lo, raw, hi_sem, hi_count, lo_sem):
                nc.gpsimd.tensor_scalar(hi, raw, 1.0, 1.0, ALU.mult, ALU.mult).then_inc(hi_sem, 1)
                pool.wait_ge(hi_sem, hi_count)
                nc.gpsimd.tensor_tensor(lo, raw, hi.bitcast(F32), ALU.subtract).then_inc(lo_sem, 1)

            def qk_split(L, i, s):
                after_alone(pool, ld_qk[s], 16 * (L * PAIRS + i + 1), pool_passed)
                after_alone(pool, proj_done, L * ITEMS + 8 * (i - 1) + 4 * s + 4, pool_passed)
                split(*ring(s, 0, QKW), raw_qk[:, QKW * s:QKW * s + QKW],
                      wqk_hi, L * H + 2 * i + s + 1, wqk_ready)

            def wo_split(L, i, s):
                after_alone(pool, ld_wo[s], 16 * (L * PAIRS + i + 1), pool_passed)
                after_alone(pool, wo_done, L * 4 * PAIRS + 4 * i, pool_passed)
                split(*ring(s, QKW, WOW), raw_wo[:, WOW * s:WOW * s + WOW],
                      wo_hi, L * H + 2 * i + s + 1, wo_ready)

            def v_low(L, i, s):
                pool.wait_ge(vs_hi, L * H + 2 * i + s + 1)
                nc.gpsimd.tensor_tensor(
                    v_l(s).rearrange("p (n f) -> p n f", n=NT),
                    v3[:, :, bass.ds(HD * (2 * i + s), HD)],
                    v_h(s).bitcast(F32).rearrange("p (n f) -> p n f", n=NT),
                    ALU.subtract).then_inc(vs_ready, 1)

            def normalise(L, i, s):
                after_alone(pool, rinv_ready, L * ITEMS + 8 * i + s + 1, pool_passed)
                for t, (a, b) in enumerate(((0, P), (P, 3 * P))):
                    q = 2 * (s % 4) + t
                    last = nc.gpsimd.tensor_scalar(pr(s)[:, a:b], pr(s)[:, a:b], rinv[:, q:q + 1],
                                                   1.0, ALU.mult, ALU.mult)
                last.then_inc(probs_ready, 1)

            def moe_gate_up(L, c, s, load):
                after_alone(pool, ld_moe[s], 16 * load, pool_passed)
                after_alone(pool, u_done, L * UNITS + 2 * c - 2, pool_passed)
                split(*ring(s, 0, 2 * D), raw_moe[:, MW * s:MW * s + 2 * D],
                      moe_hi, moe_parts(L, c, 0), gu_w_ready)

            def moe_down(L, c, s):
                after_alone(pool, down_done, L * UNITS + 2 * c - 2, pool_passed)
                split(*ring(s, 2 * D, D), raw_moe[:, MW * s + 2 * D:MW * s + MW],
                      moe_hi, moe_parts(L, c, 1), down_w_ready)

            def moe_parts(L, c, part):
                first = {(0, 0): 1, (1, 0): 2, (0, 1): 3, (1, 1): 4}
                n = first[c, part] if isinstance(c, int) and c < 2 else 2 * c + 1 + part
                return 2 * L * NCH + n

            def moe_chunk(L, c, s, load):
                moe_gate_up(L, c, s, load)
                moe_down(L, c, s)

            even, odd = NCH // 2 + 1, NCH // 2
            for L in range(2):
                if L:
                    pool.wait_ge(gout_done, 4)
                for cb in range(4):
                    pool.wait_ge(ld_wv[cb % 2], 16 * (2 * L + cb // 2 + 1))
                    raw = SP_[:, 1024 * (cb % 2):1024 * (cb % 2) + 1024]
                    split(QK[:, 2048 * cb:2048 * cb + 1024], QK[:, 2048 * cb + 1024:2048 * cb + 2048],
                          raw, wv_hi, 4 * L + cb + 1, wv_ready)
                if L:
                    pool.wait_ge(down_done, UNITS)
                qk_split(L, 0, 0)
                qk_split(L, 0, 1)
                if L == 0:
                    pool.wait_ge(ld_const, 16 * 6)
                    split(gwh[:, :], gwl[:, :], graw[:, :], gw_hi, 1, gw_ready)

                def pair(i):
                    for s in range(8):
                        if s > 0:
                            normalise(L, i, s - 1)
                        elif not is_(i, 0):
                            normalise(L, i - 1, 7)
                        if s == 0:
                            v_low(L, i, 0)
                        if s == 1 and not is_(i, PAIRS - 1):
                            qk_split(L, i + 1, 0)
                        if s == 4:
                            v_low(L, i, 1)
                        if s == 5 and not is_(i, PAIRS - 1):
                            qk_split(L, i + 1, 1)
                        if s >= 6:
                            wo_split(L, i, s - 6)
                            if is_(i, PAIRS - 1):
                                if s == 6:
                                    pool.wait_ge(proj_done, (L + 1) * ITEMS)
                                moe_gate_up(L, s - 6, s - 6, L * (even, odd)[s - 6] + 1)

                over_pairs(pool, pair)
                normalise(L, PAIRS - 1, 7)

                pool.wait_ge(wo_done, (L + 1) * 4 * PAIRS)
                moe_down(L, 0, 0)
                moe_down(L, 1, 1)
                pool.wait_ge(z_ready, NT * (3 * L + 2))
                nc.gpsimd.tensor_scalar(Y[:, :], Y[:, :], 0.5, 1.0, ALU.mult, ALU.mult)\
                    .then_inc(y_halved, 1)
                pool.wait_ge(y_halved, L + 1)
                nc.gpsimd.tensor_tensor(X[:, :], X[:, :], Y[:, :], ALU.add).then_inc(x_half, 1)
                moe_chunk(L, 2, 0, L * even + 2)
                with pool.Fori(1, NCH // 2) as r:
                    moe_chunk(L, 2 * r + 1, 1, r + (L * odd + 1))
                    moe_chunk(L, 2 * r + 2, 0, r + (L * even + 2))
                if L == 0:
                    pool.wait_ge(ld_gqkv, 16)
                    split(QK[:, 0:1536], QK[:, 1536:3072], raw_moe[:, :], gla_hi, 1, gla_w_ready)
                    pool.wait_ge(ld_gout, 16)
                    split(QK[:, 3072:3584], QK[:, 3584:4096], raw_wo[:, :], gla_hi, 2, gla_w_ready)

        @block.scalar
        def _(act):
            def squares(L, hf):
                for n in range(4 * hf, 4 * hf + 4):
                    act.wait_ge(wo_added, 4 * PAIRS * L + 4 * (PAIRS - 1) + n // 2 + 1)
                    nc.scalar.activation(squared[:, D * n:D * n + D], Y[:, D * n:D * n + D], ACT.Square,
                                         accum_out=ss[:, n:n + 1]).then_inc(ss_ready, 1)

            def hT_high(k, halves=(0, 1)):
                for q in (2 * hf + c for hf in halves for c in range(DC)):
                    hf, c = q // 2, q % 2
                    w = {0: 0, 1: DC, 3: 0, 4: DC}.get(k)
                    act.wait_ge(zT_done, 4 * k + q + 1)
                    o = hTh[:, T * c + HALF * hf:T * c + HALF * hf + HALF]
                    nc.scalar.activation(o, bank[q][:, :], ACT.Copy,
                                         scale=1.0 if w is None else lnw[:, w + c:w + c + 1])\
                        .then_inc(hT_hi, 1)

            act.wait_ge(ld_const, 16 * 6)
            for L in range(2):
                hT_high(3 * L)

                def v_block(cb):
                    for n in range(0, NT, 2):
                        act.wait_ge(v_done, L * 4 * NT + 8 * cb + n + 1)
                        nc.scalar.activation(v3[:, n, bass.ds(512 * cb, 512)],
                                             bank[4 + n % 4][:, :], ACT.Copy).then_inc(v_saved_act, 1)
                with act.Fori(0, 4) as cb:
                    v_block(cb)

                def proj_high(i, s):
                    act.wait_ge(proj_done, L * ITEMS + 8 * i + 4 + s + 1)
                    q_or_k = (q_h, k_h)[s % 2](0 if s >= 4 else 1)
                    hf = (s % 4) // 2
                    nc.scalar.activation(q_or_k[:, HALF * hf:HALF * hf + HALF], bank[s % 2][:, :],
                                         ACT.Copy).then_inc(proj_hi, 1)

                def v_high(i, s):
                    g = 2 * i + s
                    after(act, ctx_done, L * ITEMS + 8 * (i - 1) + 4 * s + 4)
                    nc.scalar.activation(v_h(s).rearrange("p (n f) -> p n f", n=NT),
                                         v3[:, :, bass.ds(HD * g, HD)], ACT.Copy).then_inc(vs_hi, 1)

                def step(i, s, late=False):
                    j = 8 * i + s
                    if not (is_(i, 0) and s < TL) and not (late and s >= TL):
                        act.wait_ge(probsT_done, L * ITEMS + j - TL + 1)
                        after(act, ctx_done, L * ITEMS + j - TL - 1)
                        nc.scalar.activation(pt_h(s - TL), bank[4 + (s - TL) % 2][:, 0:384], ACT.Copy)\
                            .then_inc(pt_hi, 1)
                    if not late:
                        act.wait_ge(masked, L * ITEMS + j + 1)
                        for t, (a, b) in enumerate(((0, P), (P, 3 * P))):
                            q = 2 * (s % 4) + t
                            last = nc.scalar.activation(pr(s)[:, a:b], sc(s)[:, a:b], ACT.Exp,
                                                        bias=nmax[:, q:q + 1], scale=-1.0,
                                                        accum_out=rsum[:, q:q + 1])
                        last.then_inc(exp_done, 1)
                        if s < 4 or not is_(i, PAIRS - 1):
                            proj_high(i, s)
                    if not (is_(i, 0) and s < CL) and not (late and s >= CL):
                        act.wait_ge(ctx_done, L * ITEMS + j - CL + 1)
                        nc.scalar.activation(ctx_slot((s - CL) % 8)[0], bank[6][:, 0:S], ACT.Copy)\
                            .then_inc(ctx_hi, 1)

                for s in range(4, 8):
                    proj_high(-1, s)
                act.wait_ge(v_saved_dve, (L + 1) * 16)
                act.wait_ge(v_saved_act, (L + 1) * 16)

                def pair(i):
                    for s in range(8):
                        step(i, s)
                        if s in (0, 4):
                            v_high(i, s // 4)

                over_pairs(act, pair)
                for s in range(CL):
                    step(PAIRS, s, late=True)

                def save_logits(hf):
                    act.wait_ge(lgT_done, 2 * L + hf + 1)
                    nc.scalar.activation(lgT[:, HALF * hf:HALF * hf + HALF], bank[hf][0:E, :],
                                         ACT.Copy).then_inc(lgT_ready, 1)

                squares(L, 0)
                hT_high(3 * L + 1, (0,))
                squares(L, 1)
                save_logits(0)
                hT_high(3 * L + 1, (1,))
                save_logits(1)

                def silu(c, hf):
                    m = L * UNITS + 2 * c + hf
                    act.wait_ge(g_done, m + 1)
                    after(act, su_ready, m - 1)
                    nc.scalar.activation(silu_t[hf], bank[(4, 7)[hf]][:, :], ACT.Silu)\
                        .then_inc(silu_ready, 1)

                def high(c, hf):
                    m = L * UNITS + 2 * c + hf
                    act.wait_ge(hw_ready, m + 1)
                    after(act, down_done, m - 1)
                    nc.scalar.activation(hh_h[hf], hw_t[hf], ACT.Copy).then_inc(hh_hi_ready, 1)

                act.wait_ge(lshift, L + 1)
                nc.scalar.activation(prob, prob, ACT.Exp).then_inc(lexp, 1)
                for c in range(2):
                    for hf in range(2):
                        silu(c, hf)
                for hf in range(2):
                    act.wait_ge(cwT_done, 2 * L + hf + 1)
                    nc.scalar.activation(cwT[:, HALF * hf:HALF * hf + HALF], cwT_bank(hf),
                                         ACT.Copy).then_inc(cwT_ready, 1)

                for c in range(3):
                    for hf in range(2):
                        if c:
                            silu(c + 1, hf)
                        high(c, hf)
                with act.Fori(1, NCH // 2 - 1) as r:
                    for q in range(2):
                        for hf in range(2):
                            silu(2 * r + 2 + q, hf)
                            high(2 * r + 1 + q, hf)
                for c in range(NCH - 2, NCH):
                    for hf in range(2):
                        if c + 1 < NCH:
                            silu(c + 1, hf)
                        high(c, hf)

                if L == 0:
                    hT_high(2)
                    for u, (c, kind, hf) in enumerate(GU):
                        if kind == 2:
                            continue
                        z = kq_before[u]
                        act.wait_ge(gu_done, u + 1)
                        after(act, gu_phi, z - 3)
                        o = slice(512 * (z % 4), 512 * (z % 4) + 512)
                        nc.scalar.activation(g_e[:, o], bank[4 + u % 4][:, :], ACT.Exp)
                        nc.scalar.activation(g_r[:, o], bank[4 + u % 4][:, :], ACT.Relu)\
                            .then_inc(gu_act, 1)
                    for c in range(DC):
                        act.wait_ge(go_ready, c + 1)
                        nc.scalar.activation(QK[:, 4096 + T * c:4096 + T * c + T],
                                             g_kv[:, T * c:T * c + T], ACT.Copy).then_inc(go_hi, 1)

        @block.vector
        def _(dve):
            v = nc.vector
            steps = [0]

            def link(instruction):
                steps[0] += 1
                instruction.then_inc(dve_step, 1)
                dve.wait_ge(dve_step, steps[0])

            def tile(a, n):
                return a[:, D * n:D * n + D]

            def rsqrt(dst, src, scale, eps, w=slice(0, NT)):
                link(v.tensor_scalar(rv[:, w], src, scale, eps, ALU.mult, ALU.add))
                link(v.tensor_scalar(ry[:, w].bitcast(I32), rv[:, w].bitcast(I32), -0.5, MAGIC,
                                     ALU.mult, ALU.add))
                for step in range(3):
                    link(v.tensor_tensor(rt[:, w], rv[:, w], ry[:, w], ALU.mult))
                    link(v.scalar_tensor_tensor(rt[:, w], rt[:, w], -0.5, ry[:, w],
                                                ALU.mult, ALU.mult))
                    link(v.scalar_tensor_tensor(dst if step == 2 else ry[:, w], rt[:, w], 1.5,
                                                ry[:, w], ALU.add, ALU.mult))

            stats3 = stats[:, :].rearrange("p (n k) -> p n k", k=6)
            mv3 = mv[:, :].rearrange("p (n k) -> p n k", k=2)

            def statistics():
                for n in range(NT):
                    last = v.bn_stats(stats3[:, n, :], tile(X, n))
                link(last)
                for n in range(NT):
                    last = v.bn_aggr(mv3[:, n, :], stats3[:, n, :])
                link(last)
                rsqrt(rstd[:, :], mv3[:, :, 1], 1.0, LN_EPS)

            def centred(dst, scale, signal):
                for n in range(NT):
                    v.tensor_scalar(dst[:, D * n:D * n + D], tile(X, n), mv3[:, n, 0:1],
                                    scale[:, n:n + 1], ALU.subtract, ALU.mult).then_inc(signal, 1)

            def hT_low(k, halves=(0, 1)):
                w = {0: 0, 1: DC, 3: 0, 4: DC}.get(k)
                for q in (2 * hf + c for hf in halves for c in range(DC)):
                    hf, c = q // 2, q % 2
                    o = slice(T * c + HALF * hf, T * c + HALF * hf + HALF)
                    dve.wait_ge(hT_hi, 4 * k + q + 1)
                    v.scalar_tensor_tensor(hTl[:, o], bank[q][:, :],
                                           1.0 if w is None else lnw[:, w + c:w + c + 1],
                                           hTh[:, o].bitcast(F32), ALU.mult, ALU.subtract)\
                        .then_inc(hT_ready, 1)

            def gating(L, gated):
                def n16(a): return a.rearrange("p (n e) -> p n e", e=E)
                def per_tile(a): return a.unsqueeze(2).broadcast_to([P, NT, E])
                logits = bank[6][:, 0:NT * E]
                dve.wait_ge(logits_done, L + 1)
                link(v.tensor_reduce(mx8[:, :], n16(logits), X_AXIS, ALU.max))
                v.tensor_tensor(n16(prob), n16(logits), per_tile(mx8[:, :]), ALU.subtract)\
                    .then_inc(lshift, 1)
                dve.wait_ge(lexp, L + 1)
                link(v.tensor_reduce(sm8[:, :], n16(prob), X_AXIS, ALU.add))
                link(v.reciprocal(rs8[:, :], sm8[:, :]))
                link(v.tensor_tensor(n16(prob), n16(prob), per_tile(rs8[:, :]), ALU.mult))
                for n in range(NT):
                    last = v.max(top8[:, 8 * n:8 * n + 8], prob[:, E * n:E * n + E])
                link(last)
                gated(0, 0, 0)
                least = top8[:, :].rearrange("p (n k) -> p n k", k=8)[:, :, TOPK - 1:TOPK]\
                    .broadcast_to([P, NT, E])
                v.tensor_tensor(n16(gt_t), n16(prob), least, ALU.is_gt)
                link(v.tensor_tensor(n16(eq_t), n16(prob), least, ALU.is_equal))
                v.tensor_reduce(cg8[:, :], n16(gt_t), X_AXIS, ALU.add)
                gated(0, 1, 0)
                link(v.tensor_tensor_scan(inc_t, seg[:, :], eq_t, 0.0, ALU.mult, ALU.add))
                link(v.tensor_tensor(n16(inc_t), n16(inc_t), per_tile(cg8[:, :]), ALU.add))
                link(v.scalar_tensor_tensor(sel_t, inc_t, float(TOPK), eq_t, ALU.is_le, ALU.mult))
                link(v.tensor_tensor(sel_t, sel_t, gt_t, ALU.add))
                link(v.tensor_tensor(prob, prob, sel_t, ALU.mult))
                gated(1, 0, 1)
                link(v.tensor_reduce(sm8[:, :], n16(prob), X_AXIS, ALU.add))
                link(v.reciprocal(rs8[:, :], sm8[:, :]))
                cwv = cw[:, :].rearrange("p (n e) -> p n e", e=EROWS)
                v.memset(cwv[:, :, E:E + SI // I], 1.0)
                v.memset(cwv[:, :, E + SI // I:EROWS], 0.0)
                link(v.tensor_tensor(cwv[:, :, 0:E], n16(prob), per_tile(rs8[:, :]), ALU.mult))
                part = cw3[:, :].rearrange("p (n a e) -> p n a e", a=3, e=EROWS)
                r1, r2 = (a.rearrange("p (n e) -> p n e", e=EROWS) for a in (rest1, rest2))
                link(v.tensor_copy(part[:, :, 0, :], cwv))
                link(v.tensor_tensor(r1, cwv, part[:, :, 0, :], ALU.subtract))
                link(v.tensor_copy(part[:, :, 1, :], r1))
                link(v.tensor_tensor(r2, r1, part[:, :, 1, :], ALU.subtract))
                v.tensor_copy(part[:, :, 2, :], r2).then_inc(cw3_ready, 1)
                gated(1, 1, 1)

            dve.wait_ge(ld_const, 16 * 6)
            for L in range(2):
                if L == 0:
                    for n in range(2):
                        dve.wait_ge(ld_x[n], 16)
                else:
                    dve.wait_ge(gout_added, 4)
                    dve.wait_ge(x_half, 1)
                statistics()
                link(v.tensor_tensor(ms[:, :], mv3[:, :, 1], rstd[:, :], ALU.mult))
                link(v.tensor_tensor(ms[:, :], ms[:, :], rstd[:, :], ALU.mult))
                rsqrt(rms[:, :], ms[:, :], 1.0, RMS_EPS)
                link(v.tensor_tensor(rms[:, :], rms[:, :], rstd[:, :], ALU.mult))
                centred(Z, rms, z_ready)
                hT_low(3 * L)
                centred(Y, rstd, y_ready)

                def v_block(cb):
                    for n in range(1, NT, 2):
                        dve.wait_ge(v_done, L * 4 * NT + 8 * cb + n + 1)
                        v.tensor_copy(v3[:, n, bass.ds(512 * cb, 512)], bank[4 + n % 4][:, :])\
                            .then_inc(v_saved_dve, 1)
                with dve.Fori(0, 4) as cb:
                    v_block(cb)

                def proj_low(i, s):
                    dve.wait_ge(proj_hi, L * ITEMS + 8 * i + 4 + s + 1)
                    slot, o = (0 if s >= 4 else 1), HALF * ((s % 4) // 2)
                    high, low = ((q_h, q_l), (k_h, k_l))[s % 2]
                    v.tensor_tensor(low(slot)[:, o:o + HALF], bank[s % 2][:, :],
                                    high(slot)[:, o:o + HALF].bitcast(F32), ALU.subtract)\
                        .then_inc(proj_ready, 1)

                def step(i, s, late=False):
                    j = 8 * i + s
                    if not (is_(i, 0) and s < 1) and not (late and s >= 1):
                        q = 2 * ((s - 1) % 4)
                        dve.wait_ge(exp_done, L * ITEMS + j)
                        v.reciprocal(rinv[:, q:q + 2], rsum[:, q:q + 2]).then_inc(rinv_ready, 1)
                    if not late:
                        after_alone(dve, scores_done, L * ITEMS + j + 1, dve_passed)
                        for t, (a, b) in enumerate(((0, P), (P, 3 * P))):
                            q = 2 * (s % 4) + t
                            last = v.tensor_tensor_reduce(
                                out=sc(s)[:, a:b], in0=bank[2 + s % 2][:, a:b], in1=mask[:, a:b],
                                scale=-SCALE, scalar=3.0e38, op0=ALU.add, op1=ALU.min,
                                accum_out=nmax[:, q:q + 1])
                        last.then_inc(masked, 1)
                    if not (is_(i, 0) and s < TL) and not (late and s >= TL):
                        t = s - TL
                        dve.wait_ge(pt_hi, L * ITEMS + j - TL + 1)
                        v.tensor_tensor(pt_l(t), bank[4 + t % 2][:, 0:384], pt_h(t).bitcast(F32),
                                        ALU.subtract).then_inc(pt_ready, 1)
                    if not late and (s < 4 or not is_(i, PAIRS - 1)):
                        proj_low(i, s)
                    if not (is_(i, 0) and s < CL) and not (late and s >= CL):
                        high, low = ctx_slot((s - CL) % 8)
                        dve.wait_ge(ctx_hi, L * ITEMS + j - CL + 1)
                        v.tensor_tensor(low, bank[6][:, 0:S], high.bitcast(F32), ALU.subtract)\
                            .then_inc(ctx_ready, 1)
                    b = s - (WL - 4)
                    if 0 <= b < 4 and not is_(i, 0):
                        dve.wait_ge(wo_done, L * 4 * PAIRS + 4 * (i - 1) + b + 1)
                        y2 = Y[:, 512 * b:512 * b + 512]
                        v.tensor_tensor(y2, bank[LATE_WO[b] if late else 7][:, :], y2, ALU.add).then_inc(wo_added, 1)

                for s in range(4, 8):
                    proj_low(-1, s)

                def pair(i):
                    for s in range(8):
                        step(i, s)

                over_pairs(dve, pair)
                def z(hf):
                    dve.wait_ge(wo_added, L * 4 * PAIRS + 4 * (PAIRS - 1) + 2 * (hf + 1))
                    dve.wait_ge(ss_ready, NT * L + 4 * (hf + 1))
                    w = slice(4 * hf, 4 * hf + 4)
                    rsqrt(rstd[:, w], ss[:, w], 1.0 / D, RMS_EPS, w)
                    for n in range(4 * hf, 4 * hf + 4):
                        v.tensor_scalar(Z[:, D * n:D * n + D], tile(Y, n), rstd[:, n:n + 1], None,
                                        ALU.mult).then_inc(z_ready, 1)

                for s in range(4):
                    step(PAIRS, s, late=True)
                z(0)
                step(PAIRS, 4, late=True)
                hT_low(3 * L + 1, (0,))
                z(1)
                hT_low(3 * L + 1, (1,))

                def gated(c, hf, slot):
                    m = L * UNITS + 2 * c + hf
                    dve.wait_ge(silu_ready, m + 1)
                    dve.wait_ge(u_done, m + 1)
                    v.tensor_tensor(su_t[2 * slot + hf], bank[up_bank(c, hf)][:, :], silu_t[hf],
                                    ALU.mult)\
                        .then_inc(su_ready, 1)

                def weighted(c, hf, slot):
                    m = L * UNITS + 2 * c + hf
                    dve.wait_ge(su_ready, m + 1)
                    dve.wait_ge(cwb_done, m + 1)
                    v.tensor_tensor(hw_t[hf], bank[6][:, :], su_t[2 * slot + hf], ALU.mult)\
                        .then_inc(hw_ready, 1)
                    dve.wait_ge(hh_hi_ready, m + 1)
                    v.tensor_tensor(hh_l[hf], hw_t[hf], hh_h[hf].bitcast(F32), ALU.subtract)\
                        .then_inc(hh_ready, 1)

                gating(L, gated)

                for c in range(3):
                    for hf in range(2):
                        if c:
                            gated(c + 1, hf, (c + 1) % 2)
                        weighted(c, hf, c % 2)
                with dve.Fori(1, NCH // 2 - 1) as r:
                    for q in range(2):
                        for hf in range(2):
                            gated(2 * r + 2 + q, hf, q)
                            weighted(2 * r + 1 + q, hf, 1 - q)
                for c in range(NCH - 2, NCH):
                    for hf in range(2):
                        if c + 1 < NCH:
                            gated(c + 1, hf, (c + 1) % 2)
                        weighted(c, hf, c % 2)
                dve.wait_ge(x_half, L + 1)
                dve.wait_ge(down_done, (L + 1) * UNITS)
                for q in range(4):
                    x2 = X[:, 512 * q:512 * q + 512]
                    v.scalar_tensor_tensor(x2, bank[q][:, :], 0.5, x2, ALU.mult, ALU.add)\
                        .then_inc(x_moe, 1)

                if L == 0:
                    dve.wait_ge(x_moe, 4)
                    statistics()
                    centred(Z, rstd, z_ready)
                    hT_low(2)
                    for u, (c, kind, hf) in enumerate(GU):
                        o = slice(T * c + HALF * hf, T * c + HALF * hf + HALF)
                        if kind < 2:
                            z = kq_before[u]
                            e = slice(512 * (z % 4), 512 * (z % 4) + 512)
                            dve.wait_ge(gu_act, z + 1)
                            v.scalar_tensor_tensor((g_k, g_q)[kind][:, o], g_e[:, e], 1.0,
                                                   g_r[:, e], ALU.min, ALU.add).then_inc(gu_phi, 1)
                            continue
                        dve.wait_ge(gu_done, u + 1)
                        dve.wait_ge(gu_phi, kq_before[u])
                        v.tensor_tensor(g_kv[:, o], bank[4 + u % 4][:, :], g_k[:, o], ALU.mult)\
                            .then_inc(gu_kv, 1)
                        if hf == 0:
                            continue
                        dve.wait_ge(gu_kv, v_before[u] + 1)
                        for b in range(NB):
                            w = slice(T * c + S * b, T * c + S * b + S)
                            v.tensor_tensor_scan(g_kvc[:, w], g_kv[:, w], g_kv[:, w], 0.0,
                                                 ALU.add, ALU.bypass)
                            last = v.tensor_tensor_scan(g_kc[:, w], g_k[:, w], g_k[:, w], 0.0,
                                                        ALU.add, ALU.bypass)
                        link(last)
                        w = slice(T * c, T * c + T)
                        v.tensor_tensor(g_kv[:, w], g_q[:, w], g_kvc[:, w], ALU.mult)
                        link(v.tensor_tensor(g_k[:, w], g_q[:, w], g_kc[:, w], ALU.mult))
                        link(v.tensor_scalar(g_k[:, w], g_k[:, w], GLA_EPS, None, ALU.add))
                        link(v.reciprocal(g_kc[:, w], g_k[:, w]))
                        v.tensor_tensor(g_kv[:, w], g_kv[:, w], g_kc[:, w], ALU.mult)\
                            .then_inc(go_ready, 1)
                    for c in range(DC):
                        w = slice(T * c, T * c + T)
                        dve.wait_ge(go_hi, c + 1)
                        v.tensor_tensor(QK[:, 6144 + T * c:6144 + T * c + T], g_kv[:, w],
                                        QK[:, 4096 + T * c:4096 + T * c + T].bitcast(F32),
                                        ALU.subtract).then_inc(go_lo, 1)
                    for q in range(4):
                        dve.wait_ge(gout_done, q + 1)
                        x2 = X[:, 512 * q:512 * q + 512]
                        v.scalar_tensor_tensor(x2, bank[q][:, :], GLA_SCALE, x2, ALU.mult, ALU.add)\
                            .then_inc(gout_added, 1)

        @block.tensor
        def _(pe):
            def exact_passes(terms):
                return [(a, b) for sh, sl, mh, ml in terms for a, b in ((sl, mh), (sh, ml), (sh, mh))]

            def product(o, terms, start=True, stop=True):
                passes = exact_passes(terms)
                for n, (a, b) in enumerate(passes):
                    last = nc.tensor.matmul(o, a, b, start=start and n == 0,
                                            stop=stop and n == len(passes) - 1,
                                            skip_group_check=not (start and stop))
                return last

            def hT(c, a, n):
                return hTh[:, T * c + a:T * c + a + n], hTl[:, T * c + a:T * c + a + n]

            def transpose_z(k, halves=(0, 1)):
                for q in (2 * hf + c for hf in halves for c in range(DC)):
                    hf, c = q // 2, q % 2
                    for n in range(4):
                        t = 4 * hf + n
                        if c == 0:
                            pe.wait_ge(z_ready, NT * k + t + 1)
                        last = nc.tensor.transpose(bank[q][:, P * n:P * n + P],
                                                   Z[:, D * t + P * c:D * t + P * c + P], ident[:, :])
                    last.then_inc(zT_done, 1)

            pe.wait_ge(ld_const, 16 * 6)
            for L in range(2):
                transpose_z(3 * L)

                def v_block(cb):
                    pe.wait_ge(wv_ready, 4 * L + cb + 1)
                    for n in range(NT):
                        if is_(cb, 0) and n in (0, 4):
                            pe.wait_ge(hT_ready, 4 * 3 * L + (2 if n == 0 else 4))
                        if not is_(cb, 0) or n >= 4:
                            pe.wait_ge((v_saved_act, v_saved_dve)[n % 2],
                                       L * 16 + 4 * cb + n // 2 - 1)
                        product(bank[4 + n % 4][:, :],
                                [(*hT(c, P * n, P),
                                  QK[:, bass.ds(2048 * cb + 512 * c, 512)],
                                  QK[:, bass.ds(2048 * cb + 1024 + 512 * c, 512)])
                                 for c in range(DC)]).then_inc(v_done, 1)
                v_block(0)
                with pe.Fori(1, 4) as cb:
                    v_block(cb)

                def proj(i, s):
                    k = L * ITEMS + 8 * i + 4 + s
                    slot, qk, hf = (0 if s >= 4 else 1), s % 2, (s % 4) // 2
                    if s % 4 == 0:
                        pe.wait_ge(wqk_ready, L * H + 2 * i + s // 4 + 2)
                    after(pe, proj_ready, k - 1)
                    product(bank[s % 2][:, :],
                            [(*ring(slot, D * qk + P * c, P), *hT(c, HALF * hf, HALF))
                             for c in range(DC)]).then_inc(proj_done, 1)

                for s in range(4, 8):
                    proj(-1, s)
                pe.wait_ge(v_saved_act, (L + 1) * 16)
                pe.wait_ge(v_saved_dve, (L + 1) * 16)

                def step(i, s, late=False):
                    j = 8 * i + s
                    if not late:
                        slot, b = s // 4, s % 4
                        if b in (0, 2):
                            pe.wait_ge(proj_ready, L * ITEMS + 8 * i + 4 * slot + b + 2)
                        after(pe, masked, L * ITEMS + j - 1)
                        o = bank[2 + s % 2]
                        for a, w, t in ((0, P, 0), (P, 2 * P, 1)):
                            q0, k0 = S * b + P * t, S * b
                            last = product(o[:, a:a + w],
                                           [(q_h(slot)[:, q0:q0 + P], q_l(slot)[:, q0:q0 + P],
                                             k_h(slot)[:, k0:k0 + w], k_l(slot)[:, k0:k0 + w])])
                        last.then_inc(scores_done, 1)
                    if not (is_(i, 0) and s < TL) and not (late and s >= TL):
                        pe.wait_ge(probs_ready, L * ITEMS + j - TL + 1)
                        after(pe, pt_ready, L * ITEMS + j - TL - 1)
                        for n in range(3):
                            last = nc.tensor.transpose(bank[4 + (s - TL) % 2][:, P * n:P * n + P],
                                                       pr(s - TL)[:, P * n:P * n + P], ident[:, :])
                        last.then_inc(probsT_done, 1)
                    if not late and (s < 4 or not is_(i, PAIRS - 1)):
                        proj(i, s)
                    if not (is_(i, 0) and s < CL) and not (late and s >= CL):
                        t = (s - CL) % 8
                        slot, b = t // 4, t % 4
                        if b == 0:
                            pe.wait_ge(vs_ready, L * H + 2 * (i - (1 if s < CL else 0)) + slot + 1)
                        pe.wait_ge(pt_ready, L * ITEMS + j - CL + 1)
                        after(pe, ctx_ready, L * ITEMS + j - CL)
                        def vt(n): return (v_h(slot)[:, P * n:P * n + P], v_l(slot)[:, P * n:P * n + P])
                        ph, pl = pt_h(t), pt_l(t)
                        product(bank[6][:, 0:S], [(*vt(2 * b), ph[:, 0:S], pl[:, 0:S])], stop=False)
                        product(bank[6][:, P:S], [(*vt(2 * b + 1), ph[:, S:384], pl[:, S:384])],
                                start=False).then_inc(ctx_done, 1)
                    b = s - (WL - 4)
                    if 0 <= b < 4 and not is_(i, 0):
                        w = L * 4 * PAIRS + 4 * (i - 1) + b
                        if b == 0:
                            pe.wait_ge(wo_ready, L * H + 2 * i)
                        pe.wait_ge(ctx_ready, L * ITEMS + 8 * (i - 1) + 4 + b + 1)
                        if not late or b in (0, 3):
                            after(pe, wo_added, w - 2 * late)
                        for t in range(2):
                            def part(g):
                                hi, lo = ctx_slot(4 * g + b)
                                return hi[:, P * t:P * t + P], lo[:, P * t:P * t + P]
                            last = product(bank[LATE_WO[b] if late else 7][:, D * t:D * t + D],
                                           [(*part(g), *ring(g, QKW, WOW)) for g in range(2)])
                        last.then_inc(wo_done, 1)

                def pair(i):
                    for s in range(8):
                        step(i, s)

                over_pairs(pe, pair)
                for s in range(WL):
                    step(PAIRS, s, late=True)

                def combine_transposes():
                    pe.wait_ge(cw3_ready, L + 1)
                    for hf in range(2):
                        for n in range(4):
                            w = 3 * EROWS * (4 * hf + n)
                            last = nc.tensor.transpose(cwT_bank(hf)[:, P * n:P * n + P],
                                                       cw3[:, w:w + 3 * EROWS], identb[:, :])
                        last.then_inc(cwT_done, 1)

                def down(c, s, hf, first):
                    m = L * UNITS + 2 * c + hf
                    if hf == 0:
                        pe.wait_ge(down_w_ready, L * NCH + c + 1)
                    pe.wait_ge(hh_ready, m + 1)
                    for t in range(4):
                        last = product(bank[2 * hf + t // 2][:, D * (t % 2):D * (t % 2) + D],
                                       [(hh_h[hf][:, P * t:P * t + P], hh_l[hf][:, P * t:P * t + P],
                                         *ring(s, 2 * D, D))], start=first and t % 2 == 0, stop=False)
                    last.then_inc(down_done, 1)

                def gate(c, s, hf):
                    m = L * UNITS + 2 * c + hf
                    if hf == 0:
                        pe.wait_ge(gu_w_ready, L * NCH + c + 1)
                    after(pe, silu_ready, m - 1)
                    product(bank[(4, 7)[hf]][:, :], [(*ring(s, P * d, P), *hT(d, HALF * hf, HALF))
                                                     for d in range(DC)]).then_inc(g_done, 1)

                def up(c, s, hf):
                    m = L * UNITS + 2 * c + hf
                    if up_bank(c, hf) == 5:
                        after(pe, su_ready, m - (2 if is_(c, 1) else 0))
                    product(bank[up_bank(c, hf)][:, :],
                            [(*ring(s, D + P * d, P), *hT(d, HALF * hf, HALF))
                             for d in range(DC)]).then_inc(u_done, 1)

                def gate_up(c, s, hf):
                    gate(c, s, hf)
                    up(c, s, hf)

                def combine(c, s, hf):
                    m = L * UNITS + 2 * c + hf
                    if is_(c, 0):
                        pe.wait_ge(cwT_ready, 2 * L + hf + 1)
                    after(pe, hw_ready, m)
                    nc.tensor.matmul(bank[6][:, :], sel[:, bass.ds(P * c, P)],
                                     cwT[:, HALF * hf:HALF * hf + HALF], start=True, stop=True)\
                        .then_inc(cwb_done, 1)
                    if hf:
                        down(c, s, 0, is_(c, 0))
                    elif not is_(c, 0):
                        down(c - 1, 1 - s, 1, is_(c, 1))

                def logits(hf):
                    pe.wait_ge(hT_ready, 4 * (3 * L + 1) + 2 * (hf + 1))
                    product(bank[hf][0:E, :],
                            [(gwh[:, E * c:E * c + E], gwl[:, E * c:E * c + E],
                              *hT(c, HALF * hf, HALF)) for c in range(DC)]).then_inc(lgT_done, 1)

                def logits_transposes(hf):
                    pe.wait_ge(lgT_ready, 2 * L + hf + 1)
                    for n in range(4 * hf, 4 * hf + 4):
                        last = nc.tensor.transpose(bank[6][:, E * n:E * n + E],
                                                   lgT[:, P * n:P * n + P], ident[0:E, 0:E])
                    return last

                transpose_z(3 * L + 1, (0,))
                if L == 0:
                    pe.wait_ge(gw_ready, 1)
                    pe.wait_ge(ld_sel, 16)
                logits(0)
                gate(0, 0, 0)
                transpose_z(3 * L + 1, (1,))
                up(0, 0, 0)
                logits_transposes(0)
                logits(1)
                gate(0, 0, 1)
                logits_transposes(1).then_inc(logits_done, 1)
                up(0, 0, 1)
                gate_up(1, 1, 0)
                gate_up(1, 1, 1)
                combine_transposes()
                combine(0, 0, 0)
                combine(0, 0, 1)
                for c in (1, 2):
                    for hf in range(2):
                        gate_up(c + 1, (c + 1) % 2, hf)
                        combine(c, c % 2, hf)
                with pe.Fori(1, NCH // 2 - 1) as r:
                    for q in range(2):
                        for hf in range(2):
                            gate_up(2 * r + 2 + q, q, hf)
                            combine(2 * r + 1 + q, 1 - q, hf)
                for c in range(NCH - 2, NCH):
                    for hf in range(2):
                        if c + 1 < NCH:
                            gate_up(c + 1, (c + 1) % 2, hf)
                        combine(c, c % 2, hf)
                down(NCH - 1, 0, 1, False)

                if L == 0:
                    transpose_z(2)
                    pe.wait_ge(gla_w_ready, 1)
                    for u, (c, kind, hf) in enumerate(GU):
                        if u in (0, 1):
                            pe.wait_ge(hT_ready, 4 * 2 + 2 * (hf + 1))
                        if u >= 4:
                            w = u - 4
                            if GU[w][1] < 2:
                                pe.wait_ge(gu_act, kq_before[w] + 1)
                            else:
                                pe.wait_ge(gu_kv, v_before[w] + 1)
                        col = (D, 0, 2 * D)[kind] + P * c
                        product(bank[4 + u % 4][:, :],
                                [(QK[:, 768 * d + col:768 * d + col + P],
                                  QK[:, 1536 + 768 * d + col:1536 + 768 * d + col + P],
                                  *hT(d, HALF * hf, HALF)) for d in range(DC)]).then_inc(gu_done, 1)
                    pe.wait_ge(gla_w_ready, 2)
                    pe.wait_ge(go_lo, DC)
                    for q in range(4):
                        for t in range(2):
                            a = P * (2 * q + t)
                            last = product(bank[q][:, D * t:D * t + D],
                                           [(QK[:, 4096 + T * c + a:4096 + T * c + a + P],
                                             QK[:, 6144 + T * c + a:6144 + T * c + a + P],
                                             QK[:, 3072 + D * c:3072 + D * c + D],
                                             QK[:, 3584 + D * c:3584 + D * c + D])
                                            for c in range(DC)])
                        last.then_inc(gout_done, 1)


def kernel(**inputs):
    import concourse.bacc as bacc
    import ml_dtypes
    from concourse.bass_utils import run_bass_kernel_spmd

    a = {n.removeprefix("L0_").removeprefix("ffn_").removeprefix("attn_"): np.asarray(v)
         for n, v in inputs.items()}

    def by_partition(w, axis_first=True):
        return np.ascontiguousarray(w.reshape(-1, P, w.shape[-1]).transpose(1, 0, 2))

    def per_head(w):
        return w.reshape(DC, P, H, HD).transpose(2, 1, 0, 3).reshape(H, P, DC * HD)

    def per_chunk(w):
        w = np.pad(w, ((0, NCH * P - UP), (0, 0)))
        return w.reshape(NCH, P, DC, P).transpose(0, 3, 2, 1).reshape(NCH, P, DC * P)

    gate = np.concatenate([a["eg_w"].reshape(E * I, D), a["sg_w"]])
    up = np.concatenate([a["eu_w"].reshape(E * I, D), a["su_w"]])
    down = np.concatenate([a["ed_w"].transpose(0, 2, 1).reshape(E * I, D), a["sd_w"].T])
    down = np.pad(down, ((0, NCH * P - UP), (0, 0))).reshape(NCH, P, D)

    causal = np.where(np.tri(P, dtype=bool), 0.0, -1e30).astype(np.float32)
    mask = np.concatenate([causal, np.zeros((P, P), np.float32), causal], 1)
    seg = np.tile((np.arange(E * NT) % E != 0).astype(np.float32), (P, 1))
    sel = (np.arange(NCH * P)[None, :] // I == np.arange(3 * EROWS)[:, None] % EROWS)
    arrays = {
        "x": a["x"].reshape(NT, P, D).transpose(1, 0, 2),
        "wqk": np.concatenate([per_head(a["wq"]), per_head(a["wk"])], 2),
        "wo": a["wo"].reshape(H, HD, D),
        "wv": by_partition(a["wv"]),
        "moe": np.concatenate([per_chunk(gate), per_chunk(up), down], 2),
        "gate": by_partition(a["gate_w"].T).reshape(P, DC * E),
        "ln": np.concatenate([a["ln1_w"].reshape(DC, P).T, a["ln2_w"].reshape(DC, P).T], 1),
        "wqkv": by_partition(a["W_qkv"].T).reshape(P, DC * 3 * D),
        "wout": by_partition(a["W_out"].T).reshape(P, DC * D),
        "ident": np.eye(P, dtype=np.float32),
        "identb": np.eye(P, dtype=ml_dtypes.bfloat16),
        "mask": mask,
        "seg": seg,
        "sel": sel.astype(ml_dtypes.bfloat16),
    }
    arrays = {n + "_dram": np.ascontiguousarray(v) for n, v in arrays.items()}
    nc = bacc.Bacc("TRN2", target_bir_lowering=False, num_devices=1)
    args = [nc.dram_tensor(n, v.shape, mybir.dt.from_np(v.dtype), kind="ExternalInput").ap()
            for n, v in arrays.items()]
    out = nc.dram_tensor("out_dram", (P, NT, D), F32, kind="ExternalOutput").ap()
    program(nc, *args, out)
    r = run_bass_kernel_spmd(nc, [arrays], core_ids=[0])
    y = r.results[0]["out_dram"]
    return np.ascontiguousarray(y.transpose(1, 0, 2)).reshape(NB, S, D)
```

```python
import numpy as np
import concourse.bass as bass
from concourse import mybir
from contextlib import ExitStack

F32 = mybir.dt.float32
F32R = mybir.dt.float32r
BF16 = mybir.dt.bfloat16
I32 = mybir.dt.int32
ALU = mybir.AluOpType
ACT = mybir.ActivationFunctionType
X_AXIS = mybir.AxisListType.X

P = 128
T, D = 1024, 256
NT, DC = T // P, D // P
NB, S = 4, 256
H, HD = 16, 128
PAIRS = H // 2
E, I, SI, TOPK = 16, 176, 352, 6
EROWS = 32
SHARED = -(-SI // P)
NCH = SHARED + E * I // P
HALF = 512
SCALE = float(HD) ** -0.5
GLA_SCALE = float(D // 16) ** -0.5
LN_EPS, RMS_EPS, GLA_EPS = 1e-5, 1e-6, 1e-9
QKW, WOW = 2 * D, D
MW = 3 * D
ITEMS = H * NB
UNITS = 2 * NCH
WUNITS = UNITS - 2 * SHARED
LATE_WO = (7, 2, 3, 7)
TL, CL, WL = 3, 4, 5
MAGIC = 1597463007.0


def program(nc, x_in, wqk_in, wo_in, wv_in, moe_in, gate_in, ln_in, wqkv_in, wout_in,
            ident_in, identb_in, mask_in, seg_in, sel_in, out):
    ctx = ExitStack()
    with ctx:
        def sb(name, cols, dt, parts=P):
            return ctx.enter_context(nc.sbuf_tensor(name, [parts, cols], dt))

        def sem(name):
            return ctx.enter_context(nc.semaphore(name))

        X = sb("X", NT * D, F32)
        Y = sb("Y", NT * D, F32)
        big = sb("big", NT * H * HD, F32)
        Z = big[:, 7168:9216]
        silu_t = [big[:, 2048 + 512 * s:2560 + 512 * s] for s in range(2)]
        su_t = [big[:, 9216 + 512 * s:9728 + 512 * s] for s in range(4)]
        hw_t = [big[:, 3584 + 512 * s:4096 + 512 * s] for s in range(2)]
        prob = big[:, 4608:4736]
        gt_t, eq_t, inc_t, sel_t = (big[:, 4736 + 128 * s:4864 + 128 * s] for s in range(4))
        rest1, rest2 = big[:, 5248:5376], big[:, 5504:5632]
        cw = big[:, 5760:5888]
        cw3 = big[:, 6016:6400].bitcast(BF16)
        cwT = big[0:3 * EROWS, 6400:6912].bitcast(BF16)
        squared = big[:, 0:2048]
        lgT = big[0:E, 11264:12288]
        g_e, g_r = big[:, 0:2048], big[:, 2048:4096]
        g_free = ([big[:, a:a + HALF] for a in range(4096, 7168, HALF)]
                  + [big[:, a:a + HALF] for a in range(9216, 16384, HALF)])
        g_k, g_q, g_kv, g_kc, g_kvc = (g_free[n::5] for n in range(5))
        v3 = big[:, :].rearrange("p (n f) -> p n f", n=NT)

        hTh, hTl = sb("hTh", DC * T, F32R), sb("hTl", DC * T, F32R)
        Wh, Wl = sb("Wh", 2 * MW, F32R), sb("Wl", 2 * MW, F32R)
        QK = sb("QK", 8 * T, F32R)
        Vs = sb("Vs", 4 * T, F32R)
        PT = sb("PT", 4 * 384, F32R)
        CA = sb("CA", 2 * T, F32R)
        CB = sb("CB", 4 * S, F32R)
        gla_qkv_h, gla_qkv_l = Vs[:, 0:1536], Vs[:, 1536:3072]
        gla_out_h, gla_out_l = Vs[:, 3072:3584], Vs[:, 3584:4096]
        SP_ = sb("SP_", 6 * 384, F32)
        raw_qk, raw_wo = sb("raw_qk", 2 * QKW, F32), sb("raw_wo", 2 * WOW, F32)
        raw_moe = sb("raw_moe", 2 * MW, F32)
        ident, identb = sb("ident", P, F32), sb("identb", P, BF16)
        mask, seg = sb("mask", 384, F32), sb("seg", P, F32)
        sel = sb("sel", (NCH - SHARED) * P, BF16, 3 * EROWS)
        lnw = sb("lnw", 2 * DC, F32)
        graw = sb("graw", DC * E, F32)
        gwh, gwl = sb("gwh", DC * E, F32R), sb("gwl", DC * E, F32R)
        def go_h(c): return PT[:, HALF * c:HALF * c + HALF]
        def go_l(c): return CB[:, HALF * c:HALF * c + HALF]
        stats, mv = sb("stats", NT * 6, F32), sb("mv", NT * 2, F32)
        ss = sb("ss", NT, F32)
        rstd, zscale, rv, ry, rt = (sb(n, NT, F32) for n in ("rstd", "zscale", "rv", "ry", "rt"))
        nmax, rsum, rinv = (sb(n, 8, F32) for n in ("nmax", "rsum", "rinv"))
        mx8, sm8, rs8, cg8 = (sb(n, NT, F32) for n in ("mx8", "sm8", "rs8", "cg8"))
        top8 = sb("top8", NT * 8, F32)

        bank = [ctx.enter_context(nc.psum_tensor(f"bank{i}", [P, 512], F32)) for i in range(8)]

        def q_h(s): return QK[:, 4096 * s:4096 * s + 1024]
        def q_l(s): return QK[:, 4096 * s + 1024:4096 * s + 2048]
        def k_h(s): return QK[:, 4096 * s + 2048:4096 * s + 3072]
        def k_l(s): return QK[:, 4096 * s + 3072:4096 * s + 4096]
        def v_h(s): return Vs[:, 2048 * s:2048 * s + 1024]
        def v_l(s): return Vs[:, 2048 * s + 1024:2048 * s + 2048]
        def sc(j): return SP_[:, 384 * (j % 2):384 * (j % 2) + 384]
        def pr(j): return SP_[:, 384 * (2 + j % 4):384 * (2 + j % 4) + 384]
        def pt_h(j): return PT[:, 768 * (j % 2):768 * (j % 2) + 384]
        def pt_l(j): return PT[:, 768 * (j % 2) + 384:768 * (j % 2) + 768]
        def ring(s, a, n): return Wh[:, MW * s + a:MW * s + a + n], Wl[:, MW * s + a:MW * s + a + n]
        hh_h = [CA[:, 1024 * s:1024 * s + 512] for s in range(2)]
        hh_l = [CA[:, 1024 * s + 512:1024 * s + 1024] for s in range(2)]

        def ctx_slot(s):
            if s < 4:
                return CA[:, S * s:S * s + S], CA[:, 1024 + S * s:1024 + S * s + S]
            c = 2 * S * (s % 2)
            return CB[:, c:c + S], CB[:, c + S:c + 2 * S]

        ld_x = [sem(f"ld_x{q}") for q in range(4)]
        ld_first, ld_const, ld_sel = sem("ld_first"), sem("ld_const"), sem("ld_sel")
        ld_wv = [sem(f"ld_wv{s}") for s in range(2)]
        ld_qk = [sem(f"ld_qk{s}") for s in range(2)]
        ld_wo = [sem(f"ld_wo{s}") for s in range(2)]
        ld_moe = [sem(f"ld_moe{s}") for s in range(2)]
        ld_gqkv, ld_gout = sem("ld_gqkv"), sem("ld_gout")
        stored = sem("stored")
        zeroed, zeros_used = sem("zeroed"), sem("zeros_used")
        pool_passed, dve_passed = sem("pool_passed"), sem("dve_passed")
        dve_step = sem("dve_step")
        y_ready, ss_ready, z_ready = sem("y_ready"), sem("ss_ready"), sem("z_ready")
        zT_done, hT_hi, hT_ready = sem("zT_done"), sem("hT_hi"), sem("hT_ready")
        wv_hi, wv_ready = sem("wv_hi"), sem("wv_ready")
        wqk_hi, wqk_ready = sem("wqk_hi"), sem("wqk_ready")
        wo_hi, wo_ready = sem("wo_hi"), sem("wo_ready")
        moe_hi, gu_w_ready, down_w_ready = sem("moe_hi"), sem("gu_w_ready"), sem("down_w_ready")
        gw_hi, gw_ready = sem("gw_hi"), sem("gw_ready")
        gla_hi, gla_w_ready = sem("gla_hi"), sem("gla_w_ready")
        v_done, v_saved = sem("v_done"), sem("v_saved")
        vs_hi, vs_ready = sem("vs_hi"), sem("vs_ready")
        proj_done, proj_hi, proj_ready = sem("proj_done"), sem("proj_hi"), sem("proj_ready")
        scores_done, masked_low, masked = sem("scores_done"), sem("masked_low"), sem("masked")
        exp_done, rinv_ready, probs_ready = sem("exp_done"), sem("rinv_ready"), sem("probs_ready")
        probsT_done, pt_hi, pt_ready = sem("probsT_done"), sem("pt_hi"), sem("pt_ready")
        ctx_done, ctx_hi, ctx_ready = sem("ctx_done"), sem("ctx_hi"), sem("ctx_ready")
        wo_done, wo_added = sem("wo_done"), sem("wo_added")
        lgT_done, lgT_ready = sem("lgT_done"), sem("lgT_ready")
        logits_done, lshift, lexp = sem("logits_done"), sem("lshift"), sem("lexp")
        cw3_ready, cwT_done, cwT_ready = sem("cw3_ready"), sem("cwT_done"), sem("cwT_ready")
        y_halved, x_half = sem("y_halved"), sem("x_half")
        g_done, silu_ready, u_done, su_ready = (
            sem("g_done"), sem("silu_ready"), sem("u_done"), sem("su_ready"))
        cwb_done, hw_ready, hh_hi_ready, hh_ready = (
            sem("cwb_done"), sem("hw_ready"), sem("hh_hi_ready"), sem("hh_ready"))
        down_done, x_moe = sem("down_done"), sem("x_moe")
        gu_done, gu_act, gu_phi, gu_kv = sem("gu_done"), sem("gu_act"), sem("gu_phi"), sem("gu_kv")
        gk_summed, g_num, g_den = sem("gk_summed"), sem("g_num"), sem("g_den")
        go_ready, go_hi, go_lo = sem("go_ready"), sem("go_hi"), sem("go_lo")
        gout_done, gout_added = sem("gout_done"), sem("gout_added")
        block = ctx.enter_context(nc.Block())


        def after(eng, sm, value):
            if not isinstance(value, int) or value > 0:
                eng.wait_ge(sm, value)

        def after_alone(eng, sm, value, passed):
            if not isinstance(value, int) or value > 0:
                eng.wait_ge(sm, value)
                eng.sem_inc(passed, 1)

        def over_pairs(eng, body):
            body(0)
            with eng.Fori(1, PAIRS - 1) as i:
                body(i)
            body(PAIRS - 1)

        def is_(i, value):
            return isinstance(i, int) and i == value

        def weighted_unit(L, c, hf):
            return L * WUNITS + 2 * (c - SHARED) + hf

        def gla_bank(u):
            return 4 + u % 4

        GROUPS = [(g // DC, g % DC) for g in range(2 * DC)]

        @block.sync
        def _(sp):
            def x_quarter(q):
                sp.dma_start(X[:, 512 * q:512 * q + 512].rearrange("p (n d) -> p n d", n=2),
                             x_in[:, 2 * q:2 * q + 2, :]).then_inc(ld_x[q], 16)

            def head(src, g):
                return src[bass.ds(g, 1), :, :].rearrange("a p f -> (a p) f")

            def qk(L, i, s):
                after(sp, wqk_ready, L * H + 2 * (i - 1) + s + 1)
                sp.dma_start(raw_qk[:, QKW * s:QKW * s + QKW], head(wqk_in, 2 * i + s))\
                    .then_inc(ld_qk[s], 16)

            def wo(L, i, s):
                after(sp, wo_ready, L * H + 2 * (i - 1) + s + 1)
                sp.dma_start(raw_wo[:, WOW * s:WOW * s + WOW], head(wo_in, 2 * i + s))\
                    .then_inc(ld_wo[s], 16)

            def chunk(L, c, s):
                after(sp, down_w_ready, L * NCH + c - 1)
                sp.dma_start(raw_moe[:, MW * s:MW * s + MW], head(moe_in, c))\
                    .then_inc(ld_moe[s], 16)

            def wv(L, cb):
                if cb >= 2:
                    sp.wait_ge(wv_ready, 4 * L + cb - 1)
                s = cb % 2
                sp.dma_start(SP_[:, 1024 * s:1024 * s + 1024].rearrange("p (c f) -> p c f", c=DC),
                             wv_in[:, :, 512 * cb:512 * cb + 512]).then_inc(ld_wv[s], 16)

            for L in range(2):
                if L == 0:
                    x_quarter(0)
                    x_quarter(1)
                    wv(0, 0)
                    x_quarter(2)
                    x_quarter(3)
                    wv(0, 1)
                qk(L, 0, 0)
                qk(L, 0, 1)
                if L == 0:
                    wv(0, 2)
                    wv(0, 3)
                    sp.wait_ge(zeros_used, 1)
                    sp.dma_start(sel[:, :], sel_in).then_inc(ld_sel, 16)
                else:
                    sp.wait_ge(gla_w_ready, 2)

                def pair(i):
                    for s in range(2):
                        wo(L, i, s)
                    if not is_(i, PAIRS - 1):
                        for s in range(2):
                            qk(L, i + 1, s)

                over_pairs(sp, pair)
                if L:
                    sp.wait_ge(gla_w_ready, 1)
                for c in range(3):
                    chunk(L, c, c % 2)
                if L == 0:
                    sp.wait_ge(probsT_done, ITEMS)
                    wv(1, 0)
                    wv(1, 1)
                for c in range(3, 7):
                    chunk(L, c, c % 2)
                    if L == 0 and c >= 5:
                        wv(1, c - 3)
                with sp.Fori(3, NCH // 2) as r:
                    chunk(L, 2 * r + 1, 1)
                    chunk(L, 2 * r + 2, 0)
                if L == 0:
                    sp.wait_ge(wo_ready, H)
                    sp.dma_start(raw_wo[:, :], wout_in).then_inc(ld_gout, 16)
                    sp.wait_ge(down_w_ready, NCH)
                    sp.dma_start(raw_moe[:, :], wqkv_in).then_inc(ld_gqkv, 16)
            for q in range(4):
                sp.wait_ge(x_moe, 4 + q + 1)
                sp.dma_start(out[:, 2 * q:2 * q + 2, :],
                             X[:, 512 * q:512 * q + 512].rearrange("p (n d) -> p n d", n=2))\
                    .then_inc(stored, 16)
            sp.wait_ge(stored, 16 * 4)

        @block.gpsimd
        def _(pool):
            def split(hi, lo, raw, hi_sem, hi_count, lo_sem):
                nc.gpsimd.tensor_scalar(hi, raw, 1.0, 1.0, ALU.mult, ALU.mult).then_inc(hi_sem, 1)
                pool.wait_ge(hi_sem, hi_count)
                nc.gpsimd.tensor_tensor(lo, raw, hi.bitcast(F32), ALU.subtract).then_inc(lo_sem, 1)

            def qk_split(L, i, s):
                after_alone(pool, ld_qk[s], 16 * (L * PAIRS + i + 1), pool_passed)
                after_alone(pool, proj_done, L * ITEMS + 8 * (i - 1) + 4 * s + 4,
                            pool_passed)
                split(*ring(s, 0, QKW), raw_qk[:, QKW * s:QKW * s + QKW],
                      wqk_hi, L * H + 2 * i + s + 1, wqk_ready)

            def wo_split(L, i, s):
                after_alone(pool, ld_wo[s], 16 * (L * PAIRS + i + 1), pool_passed)
                after_alone(pool, wo_done, L * 4 * PAIRS + 4 * i, pool_passed)
                split(*ring(s, QKW, WOW), raw_wo[:, WOW * s:WOW * s + WOW],
                      wo_hi, L * H + 2 * i + s + 1, wo_ready)

            def v_low(L, i, s):
                pool.wait_ge(vs_hi, L * H + 2 * i + s + 1)
                nc.gpsimd.tensor_tensor(
                    v_l(s).rearrange("p (n f) -> p n f", n=NT),
                    v3[:, :, bass.ds(HD * (2 * i + s), HD)],
                    v_h(s).bitcast(F32).rearrange("p (n f) -> p n f", n=NT),
                    ALU.subtract).then_inc(vs_ready, 1)

            def normalise(L, i, s):
                after_alone(pool, rinv_ready, L * ITEMS + 8 * i + s + 1, pool_passed)
                for t, (a, b) in enumerate(((0, P), (P, 3 * P))):
                    q = 2 * (s % 4) + t
                    last = nc.gpsimd.tensor_scalar(pr(s)[:, a:b], pr(s)[:, a:b], rinv[:, q:q + 1],
                                                   1.0, ALU.mult, ALU.mult)
                last.then_inc(probs_ready, 1)

            def moe_gate_up(L, c, s, load):
                after_alone(pool, ld_moe[s], 16 * load, pool_passed)
                after_alone(pool, u_done, L * UNITS + 2 * c - 2, pool_passed)
                split(*ring(s, 0, 2 * D), raw_moe[:, MW * s:MW * s + 2 * D],
                      moe_hi, moe_parts(L, c, 0), gu_w_ready)

            def moe_down(L, c, s):
                after_alone(pool, down_done, L * UNITS + 2 * c - 2, pool_passed)
                split(*ring(s, 2 * D, D), raw_moe[:, MW * s + 2 * D:MW * s + MW],
                      moe_hi, moe_parts(L, c, 1), down_w_ready)

            def moe_parts(L, c, part):
                first = {(0, 0): 1, (1, 0): 2, (0, 1): 3, (1, 1): 4}
                n = first[c, part] if isinstance(c, int) and c < 2 else 2 * c + 1 + part
                return 2 * L * NCH + n

            def moe_chunk(L, c, s, load, between=None):
                moe_gate_up(L, c, s, load)
                if between:
                    between()
                moe_down(L, c, s)

            even, odd = NCH // 2 + 1, NCH // 2
            def wv_split(L, cb):
                pool.wait_ge(ld_wv[cb % 2], 16 * (2 * L + cb // 2 + 1))
                raw = SP_[:, 1024 * (cb % 2):1024 * (cb % 2) + 1024]
                split(QK[:, 2048 * cb:2048 * cb + 1024], QK[:, 2048 * cb + 1024:2048 * cb + 2048],
                      raw, wv_hi, 4 * L + cb + 1, wv_ready)

            def denominator(g):
                pool.wait_ge(gk_summed, g + 1)
                pool.wait_ge(gu_phi, 2 * g + 2)
                nc.gpsimd.tensor_tensor(g_k[g], g_q[g], g_kc[g], ALU.mult).then_inc(g_den, 1)

            for L in range(2):
                if L == 0:
                    for cb in range(4):
                        wv_split(0, cb)
                qk_split(L, 0, 0)
                qk_split(L, 0, 1)
                if L == 0:
                    pool.wait_ge(ld_const, 16 * 4)
                    split(gwh[:, :], gwl[:, :], graw[:, :], gw_hi, 1, gw_ready)

                def pair(i):
                    for s in range(8):
                        if s > 0:
                            normalise(L, i, s - 1)
                        elif not is_(i, 0):
                            normalise(L, i - 1, 7)
                        if s == is_(i, 0):
                            v_low(L, i, 0)
                        if s == 1 and not is_(i, PAIRS - 1):
                            qk_split(L, i + 1, 0)
                        if s == 4:
                            v_low(L, i, 1)
                        if s == 5 and not is_(i, PAIRS - 1):
                            qk_split(L, i + 1, 1)
                        last = is_(i, PAIRS - 1)
                        if s in ((5, 6) if last else (6, 7)):
                            wo_split(L, i, s - (5 if last else 6))

                over_pairs(pool, pair)
                normalise(L, PAIRS - 1, 7)

                pool.wait_ge(proj_done, (L + 1) * ITEMS)
                moe_gate_up(L, 0, 0, L * even + 1)
                moe_gate_up(L, 1, 1, L * odd + 1)
                pool.wait_ge(wo_done, (L + 1) * 4 * PAIRS)
                moe_down(L, 0, 0)
                moe_down(L, 1, 1)
                pool.wait_ge(z_ready, NT * (3 * L + 2))
                nc.gpsimd.tensor_scalar(Y[:, :], Y[:, :], 0.5, 1.0, ALU.mult, ALU.mult)\
                    .then_inc(y_halved, 1)
                pool.wait_ge(y_halved, L + 1)
                nc.gpsimd.tensor_tensor(X[:, :], X[:, :], Y[:, :], ALU.add).then_inc(x_half, 1)
                moe_chunk(L, 2, 0, L * even + 2)
                for c in range(3, 7):
                    moe_chunk(L, c, c % 2, L * (even, odd)[c % 2] + c // 2 + 1,
                              between=(lambda: wv_split(1, c - 3)) if L == 0 else None)
                with pool.Fori(3, NCH // 2) as r:
                    moe_chunk(L, 2 * r + 1, 1, r + (L * odd + 1))
                    moe_chunk(L, 2 * r + 2, 0, r + (L * even + 2))
                if L == 0:
                    pool.wait_ge(ld_gqkv, 16)
                    split(gla_qkv_h, gla_qkv_l, raw_moe[:, :], gla_hi, 1, gla_w_ready)
                    pool.wait_ge(ld_gout, 16)
                    split(gla_out_h, gla_out_l, raw_wo[:, :], gla_hi, 2, gla_w_ready)
                    for g in range(2 * DC):
                        denominator(g)
                    pool.wait_ge(down_done, UNITS)

        @block.scalar
        def _(act):
            def squares(L, hf):
                for n in range(4 * hf, 4 * hf + 4):
                    act.wait_ge(wo_added, 4 * PAIRS * L + 4 * (PAIRS - 1) + n // 2 + 1)
                    nc.scalar.activation(squared[:, D * n:D * n + D], Y[:, D * n:D * n + D], ACT.Square,
                                         accum_out=ss[:, n:n + 1]).then_inc(ss_ready, 1)

            def hT_high(k, halves=(0, 1)):
                for q in (2 * hf + c for hf in halves for c in range(DC)):
                    hf, c = q // 2, q % 2
                    w = {0: 0, 1: DC, 3: 0, 4: DC}.get(k)
                    act.wait_ge(zT_done, 4 * k + q + 1)
                    o = hTh[:, T * c + HALF * hf:T * c + HALF * hf + HALF]
                    nc.scalar.activation(o, bank[q][:, :], ACT.Copy,
                                         scale=1.0 if w is None else lnw[:, w + c:w + c + 1])\
                        .then_inc(hT_hi, 1)

            def output_high(g):
                act.wait_ge(go_ready, g + 1)
                if g >= DC:
                    act.wait_ge(gout_done, 2)
                nc.scalar.activation(go_h(g % DC), g_kv[g], ACT.Copy).then_inc(go_hi, 1)

            for dst, src in ((ident, ident_in), (lnw, ln_in)):
                act.dma_start(dst[:, :], src).then_inc(ld_first, 16)
            for dst, src in ((graw, gate_in), (identb, identb_in), (mask, mask_in), (seg, seg_in)):
                act.dma_start(dst[:, :], src).then_inc(ld_const, 16)
            act.wait_ge(ld_first, 16 * 2)
            nc.scalar.activation(ss[:, 0:1], lnw[:, 0:1], ACT.Copy)
            for L in range(2):
                def v_blocks(hf, first, end, before_last=None):
                    with act.Fori(first, end) as cb:
                        for n in range(4):
                            if n == 3 and before_last:
                                before_last()
                            act.wait_ge(v_done, L * 4 * NT + 16 * hf + 4 * cb + n + 1)
                            nc.scalar.activation(v3[:, 4 * hf + n, bass.ds(512 * cb, 512)],
                                                 bank[4 + n][:, :], ACT.Copy).then_inc(v_saved, 1)

                hT_high(3 * L, (0,))
                if L:
                    act.wait_ge(gu_phi, 4 * DC)
                v_blocks(0, 0, 1)
                if L == 0:
                    hT_high(0, (1,))
                else:
                    output_high(2)
                v_blocks(0, 1, 2)
                if L:
                    output_high(3)
                v_blocks(0, 2, 3)
                v_blocks(0, 3, 4, before_last=(lambda: hT_high(3, (1,))) if L else None)
                v_blocks(1, 0, 4)

                def proj_high(i, s):
                    act.wait_ge(proj_done, L * ITEMS + 8 * i + 4 + s + 1)
                    q_or_k = (q_h, k_h)[s % 2](0 if s >= 4 else 1)
                    hf = (s % 4) // 2
                    nc.scalar.activation(q_or_k[:, HALF * hf:HALF * hf + HALF], bank[s % 2][:, :],
                                         ACT.Copy).then_inc(proj_hi, 1)

                def v_high(i, s):
                    g = 2 * i + s
                    after(act, ctx_done, L * ITEMS + 8 * (i - 1) + 4 * s + 4)
                    nc.scalar.activation(v_h(s).rearrange("p (n f) -> p n f", n=NT),
                                         v3[:, :, bass.ds(HD * g, HD)], ACT.Copy).then_inc(vs_hi, 1)

                def context_high(i, s):
                    if (is_(i, 0) and s < CL) or (is_(i, PAIRS) and s >= CL):
                        return
                    act.wait_ge(ctx_done, L * ITEMS + 8 * i + s - CL + 1)
                    nc.scalar.activation(ctx_slot((s - CL) % 8)[0], bank[6][:, 0:S], ACT.Copy)\
                        .then_inc(ctx_hi, 1)

                def step(i, s, late=False):
                    j = 8 * i + s
                    if not (is_(i, 0) and s < TL) and not (late and s >= TL):
                        act.wait_ge(probsT_done, L * ITEMS + j - TL + 1)
                        after(act, ctx_done, L * ITEMS + j - TL - 1)
                        nc.scalar.activation(pt_h(s - TL), bank[4 + (s - TL) % 2][:, 0:384], ACT.Copy)\
                            .then_inc(pt_hi, 1)
                    tail = late or (is_(i, PAIRS - 1) and s > 4)
                    if tail:
                        context_high(i, s)
                    if not late:
                        act.wait_ge(masked, L * ITEMS + j + 1)
                        for t, (a, b) in enumerate(((0, P), (P, 3 * P))):
                            q = 2 * (s % 4) + t
                            last = nc.scalar.activation(pr(s)[:, a:b], sc(s)[:, a:b], ACT.Exp,
                                                        bias=nmax[:, q:q + 1], scale=-1.0,
                                                        accum_out=rsum[:, q:q + 1])
                        last.then_inc(exp_done, 1)
                        if s < 4 or not is_(i, PAIRS - 1):
                            proj_high(i, s)
                    if not tail:
                        context_high(i, s)

                for s in range(4, 8):
                    proj_high(-1, s)
                act.wait_ge(v_saved, (L + 1) * 4 * NT)

                def pair(i):
                    for s in range(8):
                        step(i, s)
                        if s in (0, 4):
                            v_high(i, s // 4)

                over_pairs(act, pair)
                for s in range(CL):
                    step(PAIRS, s, late=True)

                def save_logits(hf):
                    act.wait_ge(lgT_done, 2 * L + hf + 1)
                    nc.scalar.activation(lgT[:, HALF * hf:HALF * hf + HALF], bank[hf][0:E, :],
                                         ACT.Copy).then_inc(lgT_ready, 1)

                def silu(c, hf):
                    m = L * UNITS + 2 * c + hf
                    act.wait_ge(g_done, m + 1)
                    after(act, su_ready, m - 1)
                    nc.scalar.activation(silu_t[hf], bank[(4, 7)[hf]][:, :], ACT.Silu)\
                        .then_inc(silu_ready, 1)

                def high(c, hf):
                    m = L * UNITS + 2 * c + hf
                    if isinstance(c, int) and c < SHARED:
                        source = su_t[2 * (c % 2) + hf]
                        act.wait_ge(su_ready, m + 1)
                    else:
                        source = hw_t[hf]
                        act.wait_ge(hw_ready, weighted_unit(L, c, hf) + 1)
                    after(act, down_done, m - 1)
                    nc.scalar.activation(hh_h[hf], source, ACT.Copy).then_inc(hh_hi_ready, 1)

                squares(L, 0)
                hT_high(3 * L + 1, (0,))
                squares(L, 1)
                save_logits(0)
                hT_high(3 * L + 1, (1,))
                silu(0, 0)
                save_logits(1)
                silu(0, 1)
                act.wait_ge(lshift, L + 1)
                nc.scalar.activation(prob, prob, ACT.Exp).then_inc(lexp, 1)
                for c in range(SHARED):
                    for hf in range(2):
                        silu(c + 1, hf)
                        high(c, hf)
                        if c == SHARED - 1 and hf == 0:
                            act.wait_ge(cwT_done, L + 1)
                            nc.scalar.activation(cwT[:, :], bank[6][0:3 * EROWS, :].bitcast(BF16),
                                                 ACT.Copy).then_inc(cwT_ready, 1)
                with act.Fori(1, NCH // 2 - 1) as r:
                    for q in range(2):
                        for hf in range(2):
                            silu(2 * r + 2 + q, hf)
                            high(2 * r + 1 + q, hf)
                for c in range(NCH - 2, NCH):
                    for hf in range(2):
                        if c + 1 < NCH:
                            silu(c + 1, hf)
                        high(c, hf)

                if L == 0:
                    for g, (hf, c) in enumerate(GROUPS):
                        if c == 0:
                            hT_high(2, (hf,))
                        if g == 2 * DC - 1:
                            output_high(0)
                            output_high(1)
                        for kind in range(2):
                            z = 2 * g + kind
                            act.wait_ge(gu_done, 3 * g + kind + 1)
                            after(act, gu_phi, z - 3)
                            o = slice(HALF * (z % 4), HALF * (z % 4) + HALF)
                            b = bank[gla_bank(3 * g + kind)]
                            nc.scalar.activation(g_e[:, o], b[:, :], ACT.Exp)
                            nc.scalar.activation(g_r[:, o], b[:, :], ACT.Relu).then_inc(gu_act, 1)

        @block.vector
        def _(dve):
            v = nc.vector
            steps = [0]

            def link(instruction):
                steps[0] += 1
                instruction.then_inc(dve_step, 1)
                dve.wait_ge(dve_step, steps[0])

            def tile(a, n):
                return a[:, D * n:D * n + D]

            def rsqrt(dst, src, scale, eps, w=slice(0, NT)):
                link(v.tensor_scalar(rv[:, w], src, scale, eps, ALU.mult, ALU.add))
                link(v.tensor_scalar(ry[:, w].bitcast(I32), rv[:, w].bitcast(I32), -0.5, MAGIC,
                                     ALU.mult, ALU.add))
                for step in range(3):
                    link(v.tensor_tensor(rt[:, w], rv[:, w], ry[:, w], ALU.mult))
                    link(v.scalar_tensor_tensor(rt[:, w], rt[:, w], -0.5, ry[:, w],
                                                ALU.mult, ALU.mult))
                    link(v.scalar_tensor_tensor(dst if step == 2 else ry[:, w], rt[:, w], 1.5,
                                                ry[:, w], ALU.add, ALU.mult))

            stats3 = stats[:, :].rearrange("p (n k) -> p n k", k=6)
            mv3 = mv[:, :].rearrange("p (n k) -> p n k", k=2)

            def token_tiles(hf):
                return range(4 * hf, 4 * hf + 4)

            def statistics(hf, loading=False):
                for n in token_tiles(hf):
                    if loading and n % 2 == 0:
                        dve.wait_ge(ld_x[n // 2], 16)
                    last = v.bn_stats(stats3[:, n, :], tile(X, n))
                link(last)
                for n in token_tiles(hf):
                    last = v.bn_aggr(mv3[:, n, :], stats3[:, n, :])
                link(last)

            def norm_scale(dst, hf, scale, eps):
                w = slice(4 * hf, 4 * hf + 4)
                rsqrt(dst[:, w], mv3[:, w, 1], scale, eps, w)

            def centred(dst, hf, scale, signal):
                for n in token_tiles(hf):
                    v.tensor_scalar(dst[:, D * n:D * n + D], tile(X, n), mv3[:, n, 0:1],
                                    scale[:, n:n + 1], ALU.subtract, ALU.mult).then_inc(signal, 1)

            def both_norms(hf):
                norm_scale(zscale, hf, 1.0 + RMS_EPS, LN_EPS * RMS_EPS)
                centred(Z, hf, zscale, z_ready)

            def residual(hf):
                norm_scale(rstd, hf, 1.0, LN_EPS)
                centred(Y, hf, rstd, y_ready)

            def hT_low(k, halves=(0, 1)):
                w = {0: 0, 1: DC, 3: 0, 4: DC}.get(k)
                for q in (2 * hf + c for hf in halves for c in range(DC)):
                    hf, c = q // 2, q % 2
                    o = slice(T * c + HALF * hf, T * c + HALF * hf + HALF)
                    dve.wait_ge(hT_hi, 4 * k + q + 1)
                    v.scalar_tensor_tensor(hTl[:, o], bank[q][:, :],
                                           1.0 if w is None else lnw[:, w + c:w + c + 1],
                                           hTh[:, o].bitcast(F32), ALU.mult, ALU.subtract)\
                        .then_inc(hT_ready, 1)

            def phi(g, kind):
                z = 2 * g + kind
                e = slice(HALF * (z % 4), HALF * (z % 4) + HALF)
                dve.wait_ge(gu_act, z + 1)
                v.scalar_tensor_tensor((g_k, g_q)[kind][g], g_e[:, e], 1.0, g_r[:, e],
                                       ALU.min, ALU.add).then_inc(gu_phi, 1)

            def products_kv(g):
                phi(g, 0)
                phi(g, 1)
                dve.wait_ge(gu_phi, 2 * g + 1)
                dve.wait_ge(gu_done, 3 * g + 3)
                v.tensor_tensor(g_kv[g], bank[gla_bank(3 * g + 2)][:, :], g_k[g], ALU.mult)\
                    .then_inc(gu_kv, 1)

            def sums(g):
                dve.wait_ge(gu_phi, 2 * g + 1)
                for b in range(0, HALF, S):
                    last = v.tensor_tensor_scan(g_kc[g][:, b:b + S], g_k[g][:, b:b + S],
                                                g_k[g][:, b:b + S], 0.0, ALU.add, ALU.bypass)
                last.then_inc(gk_summed, 1)
                dve.wait_ge(gu_kv, g + 1)
                for b in range(0, HALF, S):
                    last = v.tensor_tensor_scan(g_kvc[g][:, b:b + S], g_kv[g][:, b:b + S],
                                                g_kv[g][:, b:b + S], 0.0, ALU.add, ALU.bypass)
                link(last)
                dve.wait_ge(gu_phi, 2 * g + 2)
                v.tensor_tensor(g_kv[g], g_q[g], g_kvc[g], ALU.mult).then_inc(g_num, 1)

            def outputs(g):
                dve.wait_ge(g_den, g + 1)
                link(v.tensor_scalar(g_k[g], g_k[g], GLA_EPS, None, ALU.add))
                link(v.reciprocal(g_kc[g], g_k[g]))
                if g % DC:
                    outputs_low(g - 1)
                dve.wait_ge(g_num, g + 1)
                v.tensor_tensor(g_kv[g], g_kv[g], g_kc[g], ALU.mult).then_inc(go_ready, 1)

            def outputs_low(g):
                dve.wait_ge(go_hi, g + 1)
                v.tensor_tensor(go_l(g % DC), g_kv[g], go_h(g % DC).bitcast(F32),
                                ALU.subtract).then_inc(go_lo, 1)

            def gla_added(hf):
                if hf:
                    outputs_low(3)
                for q in (2 * hf, 2 * hf + 1):
                    dve.wait_ge(gout_done, q + 1)
                    x2 = X[:, 512 * q:512 * q + 512]
                    v.scalar_tensor_tensor(x2, bank[q][:, :], GLA_SCALE, x2, ALU.mult, ALU.add)\
                        .then_inc(gout_added, 1)
                dve.wait_ge(gout_added, 2 * (hf + 1))

            def n16(a): return a.rearrange("p (n e) -> p n e", e=E)
            def per_tile(a): return a.unsqueeze(2).broadcast_to([P, NT, E])

            def gating_shift(L):
                logits = bank[6][:, 0:NT * E]
                dve.wait_ge(logits_done, L + 1)
                link(v.tensor_reduce(mx8[:, :], n16(logits), X_AXIS, ALU.max))
                v.tensor_tensor(n16(prob), n16(logits), per_tile(mx8[:, :]), ALU.subtract)\
                    .then_inc(lshift, 1)

            def gating_softmax(L):
                dve.wait_ge(lexp, L + 1)
                link(v.tensor_reduce(sm8[:, :], n16(prob), X_AXIS, ALU.add))
                link(v.reciprocal(rs8[:, :], sm8[:, :]))
                link(v.tensor_tensor(n16(prob), n16(prob), per_tile(rs8[:, :]), ALU.mult))
                for n in range(NT):
                    last = v.max(top8[:, 8 * n:8 * n + 8], prob[:, E * n:E * n + E])
                link(last)
                least = top8[:, :].rearrange("p (n k) -> p n k", k=8)[:, :, TOPK - 1:TOPK]\
                    .broadcast_to([P, NT, E])
                v.tensor_tensor(n16(gt_t), n16(prob), least, ALU.is_gt)
                link(v.tensor_tensor(n16(eq_t), n16(prob), least, ALU.is_equal))

            def gating_choice():
                v.memset(cw3[:, :], 0.0)
                v.tensor_reduce(cg8[:, :], n16(gt_t), X_AXIS, ALU.add)
                link(v.tensor_tensor_scan(inc_t, seg[:, :], eq_t, 0.0, ALU.mult, ALU.add))
                link(v.tensor_tensor(n16(inc_t), n16(inc_t), per_tile(cg8[:, :]), ALU.add))
                link(v.scalar_tensor_tensor(sel_t, inc_t, float(TOPK), eq_t, ALU.is_le, ALU.mult))
                link(v.tensor_tensor(sel_t, sel_t, gt_t, ALU.add))
                link(v.tensor_tensor(prob, prob, sel_t, ALU.mult))

            def gating_weights():
                link(v.tensor_reduce(sm8[:, :], n16(prob), X_AXIS, ALU.add))
                link(v.reciprocal(rs8[:, :], sm8[:, :]))
                link(v.tensor_tensor(n16(cw), n16(prob), per_tile(rs8[:, :]), ALU.mult))
                part = cw3[:, :].rearrange("p (n a e) -> p n a e", a=3, e=EROWS)[:, :, :, 0:E]
                link(v.tensor_copy(part[:, :, 0, :], n16(cw)))
                link(v.tensor_tensor(n16(rest1), n16(cw), part[:, :, 0, :], ALU.subtract))
                link(v.tensor_copy(part[:, :, 1, :], n16(rest1)))
                link(v.tensor_tensor(n16(rest2), n16(rest1), part[:, :, 1, :], ALU.subtract))
                v.tensor_copy(part[:, :, 2, :], n16(rest2)).then_inc(cw3_ready, 1)

            v.memset(sel[:, 0:HALF], 0.0).then_inc(zeroed, 1)
            for L in range(2):
                if L == 0:
                    for hf in range(2):
                        statistics(hf, loading=True)
                        both_norms(hf)
                        if hf == 0:
                            dve.wait_ge(ld_first, 16 * 2)
                        hT_low(0, (hf,))
                    for hf in range(2):
                        residual(hf)
                    dve.wait_ge(ld_const, 16 * 4)
                else:
                    for hf in range(2):
                        if hf:
                            outputs(2)
                            outputs(3)
                        gla_added(hf)
                        statistics(hf)
                        both_norms(hf)
                        if hf == 0:
                            products_kv(3)
                        hT_low(3, (hf,))
                        if hf == 0:
                            sums(3)
                    residual(0)
                    residual(1)

                def proj_low(i, s):
                    dve.wait_ge(proj_hi, L * ITEMS + 8 * i + 4 + s + 1)
                    slot, o = (0 if s >= 4 else 1), HALF * ((s % 4) // 2)
                    high, low = ((q_h, q_l), (k_h, k_l))[s % 2]
                    v.tensor_tensor(low(slot)[:, o:o + HALF], bank[s % 2][:, :],
                                    high(slot)[:, o:o + HALF].bitcast(F32), ALU.subtract)\
                        .then_inc(proj_ready, 1)

                def context_low(i, s, lag):
                    if (is_(i, 0) and s < lag) or (is_(i, PAIRS) and s >= lag):
                        return
                    high, low = ctx_slot((s - lag) % 8)
                    dve.wait_ge(ctx_hi, L * ITEMS + 8 * i + s - lag + 1)
                    v.tensor_tensor(low, bank[6][:, 0:S], high.bitcast(F32), ALU.subtract)\
                        .then_inc(ctx_ready, 1)

                def add_output(i, b):
                    if 0 <= b < 4 and not is_(i, 0):
                        dve.wait_ge(wo_done, L * 4 * PAIRS + 4 * (i - 1) + b + 1)
                        y2 = Y[:, 512 * b:512 * b + 512]
                        o = bank[LATE_WO[b] if is_(i, PAIRS) else 7]
                        v.tensor_tensor(y2, o[:, :], y2, ALU.add).then_inc(wo_added, 1)

                def step(i, s, late=False):
                    j = 8 * i + s
                    if not (is_(i, 0) and s < 1) and not (late and s >= 1):
                        q = 2 * ((s - 1) % 4)
                        dve.wait_ge(exp_done, L * ITEMS + j)
                        v.reciprocal(rinv[:, q:q + 2], rsum[:, q:q + 2]).then_inc(rinv_ready, 1)
                    tail = late or (is_(i, PAIRS - 1) and s >= 4)
                    if tail and s == 4 and not late:
                        context_low(i, s, CL + 1)
                        add_output(i, s - WL + 3)
                    if not late:
                        after_alone(dve, scores_done, L * ITEMS + j + 1, dve_passed)
                        v.tensor_tensor(sc(s)[:, 0:P], bank[2 + s % 2][:, 3 * P:4 * P], mask[:, 0:P],
                                        ALU.add).then_inc(masked_low, 1)

                        def masked_scores(t, a, b, added):
                            q = 2 * (s % 4) + t
                            return v.tensor_tensor_reduce(
                                out=sc(s)[:, a:b], in0=bank[2 + s % 2][:, a:b], in1=added,
                                scale=-SCALE, scalar=3.0e38, op0=ALU.add, op1=ALU.min,
                                accum_out=nmax[:, q:q + 1])
                        masked_scores(1, P, 3 * P, mask[:, P:3 * P])
                        after_alone(dve, masked_low, L * ITEMS + j + 1, dve_passed)
                        masked_scores(0, 0, P, sc(s)[:, 0:P]).then_inc(masked, 1)
                    if not tail:
                        context_low(i, s, CL + 1)
                        add_output(i, s - WL + 3)
                    if not (is_(i, 0) and s < TL) and not (late and s >= TL):
                        t = s - TL
                        dve.wait_ge(pt_hi, L * ITEMS + j - TL + 1)
                        v.tensor_tensor(pt_l(t), bank[4 + t % 2][:, 0:384], pt_h(t).bitcast(F32),
                                        ALU.subtract).then_inc(pt_ready, 1)
                    if not late and s == 0:
                        proj_low(i - 1, 7)
                    elif not late and (s <= 4 or not is_(i, PAIRS - 1)):
                        proj_low(i, s - 1)
                    if tail:
                        context_low(i, s, CL)
                        add_output(i, s - WL + 4)

                for s in range(4, 7):
                    proj_low(-1, s)

                def pair(i):
                    for s in range(8):
                        step(i, s)

                over_pairs(dve, pair)
                def z(hf):
                    dve.wait_ge(wo_added, L * 4 * PAIRS + 4 * (PAIRS - 1) + 2 * (hf + 1))
                    dve.wait_ge(ss_ready, NT * L + 4 * (hf + 1))
                    w = slice(4 * hf, 4 * hf + 4)
                    rsqrt(rstd[:, w], ss[:, w], 1.0 / D, RMS_EPS, w)
                    for n in range(4 * hf, 4 * hf + 4):
                        v.tensor_scalar(Z[:, D * n:D * n + D], tile(Y, n), rstd[:, n:n + 1], None,
                                        ALU.mult).then_inc(z_ready, 1)

                for s in range(WL - 1):
                    step(PAIRS, s, late=True)
                z(0)
                step(PAIRS, WL - 1, late=True)
                hT_low(3 * L + 1, (0,))
                z(1)
                hT_low(3 * L + 1, (1,))

                def gated(c, hf, slot):
                    m = L * UNITS + 2 * c + hf
                    dve.wait_ge(silu_ready, m + 1)
                    dve.wait_ge(u_done, m + 1)
                    v.tensor_tensor(su_t[2 * slot + hf], bank[5][:, :], silu_t[hf],
                                    ALU.mult)\
                        .then_inc(su_ready, 1)

                def weighted(c, hf, slot):
                    w = weighted_unit(L, c, hf)
                    dve.wait_ge(su_ready, L * UNITS + 2 * c + hf + 1)
                    dve.wait_ge(cwb_done, w + 1)
                    v.tensor_tensor(hw_t[hf], bank[6][:, :], su_t[2 * slot + hf], ALU.mult)\
                        .then_inc(hw_ready, 1)
                    hidden_low(c, hf, hw_t[hf])

                def hidden_low(c, hf, source):
                    dve.wait_ge(hh_hi_ready, L * UNITS + 2 * c + hf + 1)
                    v.tensor_tensor(hh_l[hf], source, hh_h[hf].bitcast(F32), ALU.subtract)\
                        .then_inc(hh_ready, 1)

                gated(0, 0, 0)
                gating_shift(L)
                gated(0, 1, 0)
                for c in range(SHARED):
                    for hf in range(2):
                        gated(c + 1, hf, (c + 1) % 2)
                        hidden_low(c, hf, su_t[2 * (c % 2) + hf])
                        if (c, hf) == (0, 0):
                            gating_softmax(L)
                        if (c, hf) == (0, 1):
                            gating_choice()
                        if (c, hf) == (1, 0):
                            gating_weights()
                with dve.Fori(1, NCH // 2 - 1) as r:
                    for q in range(2):
                        for hf in range(2):
                            gated(2 * r + 2 + q, hf, q)
                            weighted(2 * r + 1 + q, hf, 1 - q)
                for c in range(NCH - 2, NCH):
                    for hf in range(2):
                        if c + 1 < NCH:
                            gated(c + 1, hf, (c + 1) % 2)
                        weighted(c, hf, c % 2)
                dve.wait_ge(x_half, L + 1)

                def moe_added(hf):
                    dve.wait_ge(down_done, (L + 1) * UNITS - 1 + hf)
                    for q in (2 * hf, 2 * hf + 1):
                        x2 = X[:, 512 * q:512 * q + 512]
                        v.scalar_tensor_tensor(x2, bank[q][:, :], 0.5, x2, ALU.mult, ALU.add)\
                            .then_inc(x_moe, 1)

                def gla_norm(hf):
                    statistics(hf)
                    norm_scale(rstd, hf, 1.0, LN_EPS)
                    centred(Z, hf, rstd, z_ready)

                moe_added(0)
                if L:
                    moe_added(1)

                if L == 0:
                    dve.wait_ge(x_moe, 2)
                    gla_norm(0)
                    moe_added(1)
                    hT_low(2, (0,))
                    dve.wait_ge(x_moe, 4)
                    gla_norm(1)
                    products_kv(0)
                    sums(0)
                    outputs(0)
                    hT_low(2, (1,))
                    products_kv(1)
                    sums(1)
                    outputs(1)
                    outputs_low(1)
                    products_kv(2)
                    sums(2)

        @block.tensor
        def _(pe):
            def exact_passes(terms):
                return [(a, b) for sh, sl, mh, ml in terms for a, b in ((sl, mh), (sh, ml), (sh, mh))]

            def product(o, terms, start=True, stop=True):
                passes = exact_passes(terms)
                for n, (a, b) in enumerate(passes):
                    last = nc.tensor.matmul(o, a, b, start=start and n == 0,
                                            stop=stop and n == len(passes) - 1,
                                            skip_group_check=not (start and stop))
                return last

            def hT(c, a, n):
                return hTh[:, T * c + a:T * c + a + n], hTl[:, T * c + a:T * c + a + n]

            def transpose_z(k, halves=(0, 1)):
                for q in (2 * hf + c for hf in halves for c in range(DC)):
                    hf, c = q // 2, q % 2
                    for n in range(4):
                        t = 4 * hf + n
                        if c == 0:
                            pe.wait_ge(z_ready, NT * k + t + 1)
                        last = nc.tensor.transpose(bank[q][:, P * n:P * n + P],
                                                   Z[:, D * t + P * c:D * t + P * c + P], ident[:, :])
                    last.then_inc(zT_done, 1)

            def keep_warm(n, free):
                for _ in range(n):
                    nc.tensor.matmul(bank[free][:, :], sel[:, 0:P], sel[:, 0:HALF],
                                     start=True, stop=True)

            def gla_projection(hf):
                pe.wait_ge(gla_w_ready, 2)
                for c in range(DC):
                    pe.wait_ge(go_lo, DC * hf + c + 1)
                    for q in (2 * hf, 2 * hf + 1):
                        for t in range(2):
                            a = P * (2 * (q % 2) + t)
                            last = product(bank[q][:, D * t:D * t + D],
                                           [(go_h(c)[:, a:a + P], go_l(c)[:, a:a + P],
                                             gla_out_h[:, D * c:D * c + D],
                                             gla_out_l[:, D * c:D * c + D])],
                                           start=c == 0 and t == 0, stop=c == DC - 1)
                        if c == DC - 1:
                            last.then_inc(gout_done, 1)

            pe.wait_ge(zeroed, 1)
            keep_warm(16, 4)
            nc.tensor.matmul(bank[4][:, :], sel[:, 0:P], sel[:, 0:HALF], start=True, stop=True)\
                .then_inc(zeros_used, 1)
            pe.wait_ge(ld_first, 16 * 2)
            for L in range(2):
                def v_blocks(hf, first, end, before_last=None):
                    with pe.Fori(first, end) as cb:
                        pe.wait_ge(wv_ready, cb + (4 * L + 1))
                        for n in range(4):
                            if n == 3 and before_last:
                                before_last()
                            if hf or first:
                                pe.wait_ge(v_saved, L * 4 * NT + 16 * hf + 4 * cb + n - 3)
                            product(bank[4 + n][:, :],
                                    [(*hT(c, HALF * hf + P * n, P),
                                      QK[:, bass.ds(2048 * cb + 512 * c, 512)],
                                      QK[:, bass.ds(2048 * cb + 1024 + 512 * c, 512)])
                                     for c in range(DC)]).then_inc(v_done, 1)

                if L:
                    keep_warm(30, 2)
                transpose_z(3 * L, (0,))
                if L:
                    keep_warm(8, 2)
                pe.wait_ge(hT_ready, 4 * 3 * L + 2)
                v_blocks(0, 0, 1)
                if L == 0:
                    transpose_z(0, (1,))
                v_blocks(0, 1, 2)
                if L:
                    gla_projection(1)
                v_blocks(0, 2, 3)
                v_blocks(0, 3, 4, before_last=(lambda: transpose_z(3, (1,))) if L else None)
                pe.wait_ge(hT_ready, 4 * 3 * L + 4)
                v_blocks(1, 0, 4)

                def proj(i, s):
                    k = L * ITEMS + 8 * i + 4 + s
                    slot, qk, hf = (0 if s >= 4 else 1), s % 2, (s % 4) // 2
                    if s % 4 == 0:
                        pe.wait_ge(wqk_ready, L * H + 2 * i + s // 4 + 2)
                    after(pe, proj_ready, k - 1)
                    product(bank[s % 2][:, :],
                            [(*ring(slot, D * qk + P * c, P), *hT(c, HALF * hf, HALF))
                             for c in range(DC)]).then_inc(proj_done, 1)

                for s in range(4, 8):
                    proj(-1, s)
                pe.wait_ge(v_saved, (L + 1) * 4 * NT)

                def step(i, s, late=False):
                    j = 8 * i + s
                    if not late:
                        slot, b = s // 4, s % 4
                        if b in (0, 2):
                            pe.wait_ge(proj_ready, L * ITEMS + 8 * i + 4 * slot + b + 2)
                        after(pe, masked, L * ITEMS + j - 1)
                        o = bank[2 + s % 2]
                        k0 = S * b
                        def q_tile(part, t): return part(slot)[:, k0 + P * t:k0 + P * t + P]
                        k_both = QK[:, 4096 * slot + 2048:4096 * slot + 4096].rearrange(
                            "p (a t) -> p a t", a=2)[:, :, k0:k0 + P]
                        nc.tensor.matmul(o[:, :].rearrange("p (a t) -> p a t", t=P)[:, 0:4:3, :],
                                         q_tile(q_h, 0), k_both, start=True, stop=False,
                                         skip_group_check=True)
                        nc.tensor.matmul(o[:, 0:P], q_tile(q_l, 0), k_h(slot)[:, k0:k0 + P],
                                         start=False, stop=True, skip_group_check=True)
                        product(o[:, P:3 * P],
                                [(q_tile(q_h, 1), q_tile(q_l, 1), k_h(slot)[:, k0:k0 + S],
                                  k_l(slot)[:, k0:k0 + S])]).then_inc(scores_done, 1)
                    if not (is_(i, 0) and s < TL) and not (late and s >= TL):
                        pe.wait_ge(probs_ready, L * ITEMS + j - TL + 1)
                        after(pe, pt_ready, L * ITEMS + j - TL - 1)
                        for n in range(3):
                            last = nc.tensor.transpose(bank[4 + (s - TL) % 2][:, P * n:P * n + P],
                                                       pr(s - TL)[:, P * n:P * n + P], ident[:, :])
                        last.then_inc(probsT_done, 1)
                    if not late and (s < 4 or not is_(i, PAIRS - 1)):
                        proj(i, s)
                    if not (is_(i, 0) and s < CL) and not (late and s >= CL):
                        t = (s - CL) % 8
                        slot, b = t // 4, t % 4
                        if b == 0:
                            pe.wait_ge(vs_ready, L * H + 2 * (i - (1 if s < CL else 0)) + slot + 1)
                        pe.wait_ge(pt_ready, L * ITEMS + j - CL + 1)
                        after(pe, ctx_ready, L * ITEMS + j - CL)
                        def vt(n): return (v_h(slot)[:, P * n:P * n + P], v_l(slot)[:, P * n:P * n + P])
                        ph, pl = pt_h(t), pt_l(t)
                        product(bank[6][:, 0:S], [(*vt(2 * b), ph[:, 0:S], pl[:, 0:S])], stop=False)
                        product(bank[6][:, P:S], [(*vt(2 * b + 1), ph[:, S:384], pl[:, S:384])],
                                start=False).then_inc(ctx_done, 1)
                    b = s - (WL - 4)
                    if 0 <= b < 4 and not is_(i, 0):
                        w = L * 4 * PAIRS + 4 * (i - 1) + b
                        if b == 0:
                            pe.wait_ge(wo_ready, L * H + 2 * i)
                        pe.wait_ge(ctx_ready, L * ITEMS + 8 * (i - 1) + 4 + b + 1)
                        if not late or b in (0, 3):
                            after(pe, wo_added, w - 2 * late)
                        for t in range(2):
                            def part(g):
                                hi, lo = ctx_slot(4 * g + b)
                                return hi[:, P * t:P * t + P], lo[:, P * t:P * t + P]
                            last = product(bank[LATE_WO[b] if late else 7][:, D * t:D * t + D],
                                           [(*part(g), *ring(g, QKW, WOW)) for g in range(2)])
                        last.then_inc(wo_done, 1)

                def pair(i):
                    for s in range(8):
                        step(i, s)

                over_pairs(pe, pair)
                for s in range(WL):
                    step(PAIRS, s, late=True)

                def combine_transposes():
                    pe.wait_ge(cw3_ready, L + 1)
                    o = bank[6][0:3 * EROWS, :].bitcast(BF16)
                    for n in range(NT):
                        last = nc.tensor.transpose(o[:, P * n:P * n + P],
                                                   cw3[:, 3 * EROWS * n:3 * EROWS * n + 3 * EROWS],
                                                   identb[:, :])
                    last.then_inc(cwT_done, 1)

                def down(c, s, hf, first):
                    m = L * UNITS + 2 * c + hf
                    if hf == 0:
                        pe.wait_ge(down_w_ready, L * NCH + c + 1)
                    pe.wait_ge(hh_ready, m + 1)
                    for t in range(4):
                        last = product(bank[2 * hf + t // 2][:, D * (t % 2):D * (t % 2) + D],
                                       [(hh_h[hf][:, P * t:P * t + P], hh_l[hf][:, P * t:P * t + P],
                                         *ring(s, 2 * D, D))], start=first and t % 2 == 0, stop=False)
                    last.then_inc(down_done, 1)

                def gate(c, s, hf):
                    m = L * UNITS + 2 * c + hf
                    if hf == 0:
                        pe.wait_ge(gu_w_ready, L * NCH + c + 1)
                    after(pe, silu_ready, m - 1)
                    product(bank[(4, 7)[hf]][:, :], [(*ring(s, P * d, P), *hT(d, HALF * hf, HALF))
                                                     for d in range(DC)]).then_inc(g_done, 1)

                def up(c, s, hf):
                    m = L * UNITS + 2 * c + hf
                    after(pe, su_ready, m)
                    product(bank[5][:, :],
                            [(*ring(s, D + P * d, P), *hT(d, HALF * hf, HALF))
                             for d in range(DC)]).then_inc(u_done, 1)

                def gate_up(c, s, hf):
                    gate(c, s, hf)
                    up(c, s, hf)

                def combine(c, s, hf):
                    if not (isinstance(c, int) and c < SHARED):
                        if is_(c, SHARED):
                            pe.wait_ge(cwT_ready, L + 1)
                        after(pe, hw_ready, weighted_unit(L, c, hf))
                        nc.tensor.matmul(bank[6][:, :], sel[:, bass.ds(P * (c - SHARED), P)],
                                         cwT[:, HALF * hf:HALF * hf + HALF], start=True, stop=True)\
                            .then_inc(cwb_done, 1)
                    if hf:
                        down(c, s, 0, is_(c, 0))
                    elif not is_(c, 0):
                        down(c - 1, 1 - s, 1, is_(c, 1))

                def logits(hf):
                    pe.wait_ge(hT_ready, 4 * (3 * L + 1) + 2 * (hf + 1))
                    product(bank[hf][0:E, :],
                            [(gwh[:, E * c:E * c + E], gwl[:, E * c:E * c + E],
                              *hT(c, HALF * hf, HALF)) for c in range(DC)]).then_inc(lgT_done, 1)

                def logits_transposes(hf):
                    pe.wait_ge(lgT_ready, 2 * L + hf + 1)
                    for n in range(4 * hf, 4 * hf + 4):
                        last = nc.tensor.transpose(bank[6][:, E * n:E * n + E],
                                                   lgT[:, P * n:P * n + P], ident[0:E, 0:E])
                    return last

                if L == 0:
                    pe.wait_ge(gw_ready, 1)
                    pe.wait_ge(ld_sel, 16)
                    pe.wait_ge(ld_const, 16 * 4)
                keep_warm(8, 4)
                transpose_z(3 * L + 1, (0,))
                keep_warm(8, 4)
                logits(0)
                gate(0, 0, 0)
                transpose_z(3 * L + 1, (1,))
                up(0, 0, 0)
                logits_transposes(0)
                logits(1)
                gate(0, 0, 1)
                logits_transposes(1).then_inc(logits_done, 1)
                up(0, 0, 1)
                for c in range(SHARED):
                    for hf in range(2):
                        gate_up(c + 1, (c + 1) % 2, hf)
                        combine(c, c % 2, hf)
                        if c == SHARED - 1 and hf == 0:
                            combine_transposes()
                with pe.Fori(1, NCH // 2 - 1) as r:
                    for q in range(2):
                        for hf in range(2):
                            gate_up(2 * r + 2 + q, q, hf)
                            combine(2 * r + 1 + q, 1 - q, hf)
                for c in range(NCH - 2, NCH):
                    for hf in range(2):
                        if c + 1 < NCH:
                            gate_up(c + 1, (c + 1) % 2, hf)
                        combine(c, c % 2, hf)
                down(NCH - 1, 0, 1, False)

                if L == 0:
                    for g, (hf, c) in enumerate(GROUPS):
                        if c == 0:
                            keep_warm(16 if hf == 0 else 6, 4 if hf == 0 else 0)
                            transpose_z(2, (hf,))
                            keep_warm(7 if hf == 0 else 18, 4 if hf == 0 else 0)
                            pe.wait_ge(gla_w_ready, 1)
                            pe.wait_ge(hT_ready, 4 * 2 + 2 * (hf + 1))
                        for kind in range(3):
                            u = 3 * g + kind
                            if u == 6 * DC - 1:
                                keep_warm(7, 0)
                                gla_projection(0)
                            if u >= 4:
                                w = u - 4
                                if w % 3 < 2:
                                    pe.wait_ge(gu_act, 2 * (w // 3) + w % 3 + 1)
                                else:
                                    pe.wait_ge(gu_kv, w // 3 + 1)
                            col = (D, 0, 2 * D)[kind] + P * c
                            product(bank[gla_bank(u)][:, :],
                                    [(gla_qkv_h[:, 768 * d + col:768 * d + col + P],
                                      gla_qkv_l[:, 768 * d + col:768 * d + col + P],
                                      *hT(d, HALF * hf, HALF)) for d in range(DC)])\
                                .then_inc(gu_done, 1)


def kernel(**inputs):
    import concourse.bacc as bacc
    import ml_dtypes
    from concourse.bass_utils import run_bass_kernel_spmd

    a = {n.removeprefix("L0_").removeprefix("ffn_").removeprefix("attn_"): np.asarray(v)
         for n, v in inputs.items()}

    def by_partition(w):
        return np.ascontiguousarray(w.reshape(-1, P, w.shape[-1]).transpose(1, 0, 2))

    def per_head(w):
        return w.reshape(DC, P, H, HD).transpose(2, 1, 0, 3).reshape(H, P, DC * HD)

    def per_chunk(w):
        return w.reshape(NCH, P, DC, P).transpose(0, 3, 2, 1).reshape(NCH, P, DC * P)

    def shared_first(shared, experts):
        return np.concatenate([np.pad(shared, ((0, SHARED * P - SI), (0, 0))),
                               experts.reshape(E * I, D)])

    gate = shared_first(a["sg_w"], a["eg_w"])
    up = shared_first(a["su_w"], a["eu_w"])
    down = shared_first(a["sd_w"].T, a["ed_w"].transpose(0, 2, 1)).reshape(NCH, P, D)

    causal = np.where(np.tri(P, dtype=bool), 0.0, -1e30).astype(np.float32)
    mask = np.concatenate([causal, np.zeros((P, P), np.float32), causal], 1)
    seg = np.tile((np.arange(E * NT) % E != 0).astype(np.float32), (P, 1))
    sel = np.arange(E * I)[None, :] // I == np.arange(3 * EROWS)[:, None] % EROWS
    arrays = {
        "x": a["x"].reshape(NT, P, D).transpose(1, 0, 2),
        "wqk": np.concatenate([per_head(a["wq"]), per_head(a["wk"])], 2),
        "wo": a["wo"].reshape(H, HD, D),
        "wv": by_partition(a["wv"]),
        "moe": np.concatenate([per_chunk(gate), per_chunk(up), down], 2),
        "gate": by_partition(a["gate_w"].T).reshape(P, DC * E),
        "ln": np.concatenate([a["ln1_w"].reshape(DC, P).T, a["ln2_w"].reshape(DC, P).T], 1),
        "wqkv": by_partition(a["W_qkv"].T).reshape(P, DC * 3 * D),
        "wout": by_partition(a["W_out"].T).reshape(P, DC * D),
        "ident": np.eye(P, dtype=np.float32),
        "identb": np.eye(P, dtype=ml_dtypes.bfloat16),
        "mask": mask,
        "seg": seg,
        "sel": sel.astype(ml_dtypes.bfloat16),
    }
    arrays = {n + "_dram": np.ascontiguousarray(v) for n, v in arrays.items()}
    nc = bacc.Bacc("TRN2", target_bir_lowering=False, num_devices=1)
    args = [nc.dram_tensor(n, v.shape, mybir.dt.from_np(v.dtype), kind="ExternalInput").ap()
            for n, v in arrays.items()]
    out = nc.dram_tensor("out_dram", (P, NT, D), F32, kind="ExternalOutput").ap()
    program(nc, *args, out)
    r = run_bass_kernel_spmd(nc, [arrays], core_ids=[0])
    y = r.results[0]["out_dram"]
    return np.ascontiguousarray(y.transpose(1, 0, 2)).reshape(NB, S, D)
```
